# Optimizing a Trainium2 kernel written in Bass

```python
import numpy as np
import jax
import jax.numpy as jnp

def _softmax(x, axis=-1):
    return jax.nn.softmax(x, axis=axis)

def _gelu(x):
    return jax.nn.gelu(x, approximate=True)

def _silu(x):
    return jax.nn.silu(x)

def _sigmoid(x):
    return jax.nn.sigmoid(x)

def _layernorm(x, axis=-1, eps=1e-05):
    m = jnp.mean(x, axis=axis, keepdims=True)
    v = jnp.var(x, axis=axis, keepdims=True)
    return (x - m) / jnp.sqrt(v + eps)

def _scatter_add(tgt, idx, src, axis=0):
    return tgt.at[idx].add(src)

def _segment_sum(src, seg, n):
    return jax.ops.segment_sum(src, seg, n)
kernel_name = 'mk_decoder_preln_d1_seqx_r8_1fac6d'

def setup_inputs(seed: int=0):
    np.random.seed(seed)
    _w = jnp.asarray

    def _rec_inputs():
        import jax
        import jax.numpy as jnp
        _rk = jax.random.key(seed)
        x = 0.0002417 + 0.9998 * jax.random.normal(jax.random.fold_in(_rk, 1), (4, 512, 128), jnp.float32)
        _lenS = 512 - jax.random.randint(jax.random.fold_in(_rk, 7), (4,), 0, max(1, 512 // 4) + 1, jnp.int32)
        _lenS2 = 77 - jax.random.randint(jax.random.fold_in(_rk, 8), (4,), 0, max(1, 77 // 4) + 1, jnp.int32)
        _ctx_1024P = jax.random.normal(jax.random.fold_in(_rk, 11), (4, 16, 128), jnp.float32)
        _ctx_1024c = jax.random.dirichlet(jax.random.fold_in(_rk, 511), 0.3 * jnp.ones((16,), jnp.float32), (4, 77))
        _ctx_1024t = jnp.einsum('bsk,bkd->bsd', _ctx_1024c, _ctx_1024P)
        _ctx_1024t = _ctx_1024t * jax.lax.rsqrt(jnp.mean(jnp.square(_ctx_1024t)) + 1e-12) * 0.953939
        ctx_1024 = 7.22013e-05 + 1.00017 * (_ctx_1024t + 0.3 * jax.random.normal(jax.random.fold_in(_rk, 611), (4, 77, 128), jnp.float32))
        return (x, ctx_1024)
    x, ctx_1024 = _rec_inputs()

    def _L0_attn_setup():
        import jax, jax.numpy as jnp
        import numpy as np
        B, N, D_IN, D_OUT, H = (2, 256, 128, 128, 16)
        HEAD_DIM = D_OUT // H
        key = jax.random.key(seed)
        ks = jax.random.split(key, 8)
        s = 0.02
        return {'x': jax.random.normal(ks[0], (B, N, D_IN), dtype=jnp.float32), 'Wq': jax.random.normal(ks[1], (D_IN, D_OUT), dtype=jnp.float32) * s, 'Wk': jax.random.normal(ks[2], (D_IN, D_OUT), dtype=jnp.float32) * s, 'Wv': jax.random.normal(ks[3], (D_IN, D_OUT), dtype=jnp.float32) * s, 'Wo': jax.random.normal(ks[4], (D_OUT, D_OUT), dtype=jnp.float32) * s, 'bo': jnp.zeros((D_OUT,), dtype=jnp.float32), 'w': jax.random.uniform(ks[5], (H,), dtype=jnp.float32), 'v': jax.random.uniform(ks[6], (H,), dtype=jnp.float32)}
    _L0_attn_all = _L0_attn_setup()
    _L0_attn_in = {k: v for k, v in _L0_attn_all.items() if k in ('Wq', 'Wk', 'Wv', 'Wo', 'bo', 'w', 'v')}
    del _L0_attn_all

    def _L0_xattn_setup():
        import jax, jax.numpy as jnp
        import numpy as np
        D_MODEL = 128
        B, S = (4, 256)
        key = jax.random.key(seed)
        ks = jax.random.split(key, 10)
        s = 1.0 / np.sqrt(D_MODEL)
        return {'k': jax.random.normal(ks[0], (B, S, D_MODEL), jnp.float32), 'v': jax.random.normal(ks[1], (B, S, D_MODEL), jnp.float32), 'q': jax.random.normal(ks[2], (B, S, D_MODEL), jnp.float32), 'Wk': jax.random.normal(ks[3], (D_MODEL, D_MODEL), jnp.float32) * s, 'Wv': jax.random.normal(ks[4], (D_MODEL, D_MODEL), jnp.float32) * s, 'bv': jnp.zeros((D_MODEL,), jnp.float32), 'Wq': jax.random.normal(ks[5], (D_MODEL, D_MODEL), jnp.float32) * s, 'bq': jnp.zeros((D_MODEL,), jnp.float32), 'Wo': jax.random.normal(ks[6], (D_MODEL, D_MODEL), jnp.float32) * s, 'bo': jnp.zeros((D_MODEL,), jnp.float32)}
    _L0_xattn_all = _L0_xattn_setup()
    _L0_xattn_in = {k: v for k, v in _L0_xattn_all.items() if k in ('Wk', 'Wv', 'bv', 'Wq', 'bq', 'Wo', 'bo')}
    del _L0_xattn_all

    def _L0_ffn_setup():
        import jax, jax.numpy as jnp
        import numpy as np
        MICRO_BATCHES = 2
        TOP_K = 2
        NUM_EXPERTS = 8
        B, S, D = (4, 512, 128)
        H = 4 * D
        key = jax.random.key(seed)
        ks = jax.random.split(key, 8)
        s = 0.02
        return {'x': jax.random.normal(ks[0], (B, S, D), jnp.float32), 'ln_scale': jnp.ones((D,), jnp.float32), 'ln_bias': jnp.zeros((D,), jnp.float32), 'attn_w': jax.random.normal(ks[1], (D, D), jnp.float32) * s, 'attn_b': jnp.zeros((D,), jnp.float32), 'gate_w': jax.random.normal(ks[2], (NUM_EXPERTS, D), jnp.float32) * s, 'w1': jax.random.normal(ks[3], (NUM_EXPERTS, D, H), jnp.float32) * s, 'b1': jnp.zeros((NUM_EXPERTS, H), jnp.float32), 'w2': jax.random.normal(ks[4], (NUM_EXPERTS, H, D), jnp.float32) * s, 'b2': jnp.zeros((NUM_EXPERTS, D), jnp.float32), 'next_w': jax.random.normal(ks[5], (D, D), jnp.float32) * s, 'next_b': jnp.zeros((D,), jnp.float32)}
    _L0_ffn_all = _L0_ffn_setup()
    _L0_ffn_in = {k: v for k, v in _L0_ffn_all.items() if k in ('ln_scale', 'ln_bias', 'attn_w', 'attn_b', 'gate_w', 'w1', 'b1', 'w2', 'b2', 'next_w', 'next_b')}
    del _L0_ffn_all
    return {'x': x, 'ctx_1024': ctx_1024, 'L0_attn_Wq': _L0_attn_in['Wq'], 'L0_attn_Wk': _L0_attn_in['Wk'], 'L0_attn_Wv': _L0_attn_in['Wv'], 'L0_attn_Wo': _L0_attn_in['Wo'], 'L0_attn_bo': _L0_attn_in['bo'], 'L0_attn_w': _L0_attn_in['w'], 'L0_attn_v': _L0_attn_in['v'], 'L0_xattn_Wk': _L0_xattn_in['Wk'], 'L0_xattn_Wv': _L0_xattn_in['Wv'], 'L0_xattn_bv': _L0_xattn_in['bv'], 'L0_xattn_Wq': _L0_xattn_in['Wq'], 'L0_xattn_bq': _L0_xattn_in['bq'], 'L0_xattn_Wo': _L0_xattn_in['Wo'], 'L0_xattn_bo': _L0_xattn_in['bo'], 'L0_ffn_ln_scale': _L0_ffn_in['ln_scale'], 'L0_ffn_ln_bias': _L0_ffn_in['ln_bias'], 'L0_ffn_attn_w': _L0_ffn_in['attn_w'], 'L0_ffn_attn_b': _L0_ffn_in['attn_b'], 'L0_ffn_gate_w': _L0_ffn_in['gate_w'], 'L0_ffn_w1': _L0_ffn_in['w1'], 'L0_ffn_b1': _L0_ffn_in['b1'], 'L0_ffn_w2': _L0_ffn_in['w2'], 'L0_ffn_b2': _L0_ffn_in['b2'], 'L0_ffn_next_w': _L0_ffn_in['next_w'], 'L0_ffn_next_b': _L0_ffn_in['next_b']}

def reference(x, ctx_1024, L0_attn_Wq, L0_attn_Wk, L0_attn_Wv, L0_attn_Wo, L0_attn_bo, L0_attn_w, L0_attn_v, L0_xattn_Wk, L0_xattn_Wv, L0_xattn_bv, L0_xattn_Wq, L0_xattn_bq, L0_xattn_Wo, L0_xattn_bo, L0_ffn_ln_scale, L0_ffn_ln_bias, L0_ffn_attn_w, L0_ffn_attn_b, L0_ffn_gate_w, L0_ffn_w1, L0_ffn_b1, L0_ffn_w2, L0_ffn_b2, L0_ffn_next_w, L0_ffn_next_b):
    import jax
    import jax.numpy as jnp

    def _L0_attn_ref(x, Wq, Wk, Wv, Wo, bo, w, v):
        import jax, jax.numpy as jnp
        import numpy as np
        B, N, D_IN, D_OUT, H = (2, 256, 128, 128, 16)
        HEAD_DIM = D_OUT // H
        b, n, _ = x.shape
        h = w.shape[0]
        hd = Wq.shape[1] // h

        def proj(W):
            return (x @ W).reshape(b, n, h, hd).transpose(0, 2, 1, 3)
        q, k, val = (proj(Wq), proj(Wk), proj(Wv))
        pos = jnp.arange(n)
        R = jnp.abs(pos[:, None] - pos[None, :]).astype(x.dtype)
        wv = w[:, None, None]
        vv = v[:, None, None]
        R_hat = (1.0 + jnp.exp(vv)) / (1.0 + jnp.exp(vv - wv * R))
        scores = jax.nn.relu(jnp.einsum('bhqd,bhkd->bhqk', q, k)) * R_hat[None]
        causal = jnp.triu(jnp.ones((n, n), dtype=bool), k=1)
        scores = jnp.where(causal[None, None], -jnp.inf, scores)
        attn = jax.nn.softmax(scores / np.sqrt(hd).astype(x.dtype), axis=-1)
        ctx = jnp.einsum('bhqk,bhkd->bhqd', attn, val)
        ctx = ctx.transpose(0, 2, 1, 3).reshape(b, n, h * hd)
        return ctx @ Wo + bo

    def _L0_xattn_ref(k, v, q, Wk, Wv, bv, Wq, bq, Wo, bo):
        import jax, jax.numpy as jnp
        import numpy as np
        D_MODEL = 128
        B, S = (4, 256)
        kp = jnp.einsum('bsd,ed->bse', k, Wk)
        vp = jnp.einsum('bsd,ed->bse', v, Wv) + bv
        qp = jnp.einsum('bsd,ed->bse', q, Wq) + bq
        scale = 1.0 / jnp.sqrt(jnp.float32(kp.shape[-1]))
        scores = jnp.einsum('bqd,bkd->bqk', qp, kp) * scale
        probs = jax.nn.softmax(scores, axis=-1)
        ctx = jnp.einsum('bqk,bkd->bqd', probs, vp)
        return jnp.einsum('bqd,ed->bqe', ctx, Wo) + bo

    def _L0_ffn_ref(x, ln_scale, ln_bias, attn_w, attn_b, gate_w, w1, b1, w2, b2, next_w, next_b):
        import jax, jax.numpy as jnp
        import numpy as np
        MICRO_BATCHES = 2
        TOP_K = 2
        NUM_EXPERTS = 8
        B, S, D = (4, 512, 128)
        H = 4 * D
        b, s, d = x.shape
        flat = x.reshape(b * s, d)
        mu = jnp.mean(flat, axis=-1, keepdims=True)
        var = jnp.mean((flat - mu) ** 2, axis=-1, keepdims=True)
        xn = (flat - mu) * jax.lax.rsqrt(var + 1e-05) * ln_scale + ln_bias
        x_attn = xn @ attn_w.T + attn_b + flat
        logits = x_attn @ gate_w.T
        _vals, _idx = jax.lax.top_k(logits, TOP_K)
        e = w1.shape[0]
        n = b * s // (MICRO_BATCHES * e)
        xe = x_attn.reshape(MICRO_BATCHES, e, n, d)
        h = jax.nn.gelu(jnp.einsum('mend,edh->menh', xe, w1) + b1[None, :, None, :], approximate=False)
        eo = jnp.einsum('menh,ehd->mend', h, w2) + b2[None, :, None, :]
        eo = eo.reshape(b * s, d)
        out = jax.nn.gelu(eo @ next_w.T + next_b, approximate=False)
        return out.reshape(b, s, d)
    x = x + _L0_attn_ref(_layernorm(x, axis=-1), L0_attn_Wq, L0_attn_Wk, L0_attn_Wv, L0_attn_Wo, L0_attn_bo, L0_attn_w, L0_attn_v)
    x = x + _L0_xattn_ref(ctx_1024, ctx_1024, _layernorm(x, axis=-1), L0_xattn_Wk, L0_xattn_Wv, L0_xattn_bv, L0_xattn_Wq, L0_xattn_bq, L0_xattn_Wo, L0_xattn_bo)
    x = x + _L0_ffn_ref(_layernorm(x, axis=-1), L0_ffn_ln_scale, L0_ffn_ln_bias, L0_ffn_attn_w, L0_ffn_attn_b, L0_ffn_gate_w, L0_ffn_w1, L0_ffn_b1, L0_ffn_w2, L0_ffn_b2, L0_ffn_next_w, L0_ffn_next_b)
    return x

_drawn_inputs = setup_inputs


def setup_inputs(seed=0):
    import zlib

    import numpy as np

    out = dict(_drawn_inputs(seed))
    spreads = {'L0_attn_bo': (0.0, 0.334),
     'L0_xattn_bv': (0.0, 0.284),
     'L0_xattn_bq': (0.0, 1.034),
     'L0_xattn_bo': (0.0, 0.393),
     'L0_ffn_ln_scale': (1.0, 0.6),
     'L0_ffn_ln_bias': (0.0, 0.8),
     'L0_ffn_attn_b': (0.0, 0.8),
     'L0_ffn_b1': (0.0, 0.8),
     'L0_ffn_b2': (0.0, 0.8),
     'L0_ffn_next_b': (0.0, 0.8)}
    factors = {'L0_attn_Wq': 8.0,
     'L0_attn_Wk': 8.0,
     'L0_attn_Wv': 8.0,
     'L0_attn_Wo': 8.0,
     'L0_attn_w': 8.0,
     'L0_attn_v': 8.0,
     'L0_ffn_attn_w': 8.0,
     'L0_ffn_w1': 8.0,
     'L0_ffn_w2': 8.0,
     'L0_ffn_next_w': 5.122}
    for name, (base, spread) in spreads.items():
        noise = np.random.default_rng([zlib.crc32(name.encode()), seed]).standard_normal(out[name].shape)
        drawn = base * np.exp(spread * noise) if base else spread * noise
        out[name] = jnp.asarray(drawn.astype(out[name].dtype))
    for name, factor in factors.items():
        out[name] = (out[name] * factor).astype(out[name].dtype)
    return out
```

```python
from contextlib import ExitStack

import concourse.bass as bass
from concourse import mybir

ALU = mybir.AluOpType
ACT = mybir.ActivationFunctionType
AX = mybir.AxisListType
F32 = mybir.dt.float32
BF16 = mybir.dt.bfloat16

P = 128
LN_EPS = 1e-5
Q_PART = (0, 0, 1, 0, 2, 1)
K_PART = (0, 1, 0, 2, 0, 1)
SLOTS = len(Q_PART)
ROW_B1, ROW_B2, ROW_XBQ, ROW_LN_SCALE, ROW_LN_BIAS, ROW_ATTN_B, VEC_ROWS = 0, 32, 40, 41, 42, 43, 44


def decoder_kernel(nc, x, ctx_1024, L0_attn_Wq, L0_attn_Wk, L0_attn_Wv, L0_attn_Wo, L0_attn_bo, L0_attn_w,
                   L0_attn_v, L0_xattn_Wk, L0_xattn_Wv, L0_xattn_bv, L0_xattn_Wq, L0_xattn_bq, L0_xattn_Wo,
                   L0_xattn_bo, L0_ffn_ln_scale, L0_ffn_ln_bias, L0_ffn_attn_w, L0_ffn_attn_b, L0_ffn_w1,
                   L0_ffn_b1, L0_ffn_w2, L0_ffn_b2, L0_ffn_next_w, L0_ffn_next_b, out):
    B, N, D = x.shape
    H = L0_attn_w.shape[0]
    HD = D // H
    CL = ctx_1024.shape[1]
    E, _, FF = L0_ffn_w1.shape
    QT = N // P
    T = B * QT
    FC = FF // P
    HG = 4
    G = H // HG
    UNITS = G * QT
    STEPS = UNITS * HG
    VW = HD + 1
    MB = T // E
    STRIP = N + P
    SCORE_SCALE = 1.0 / float(HD) ** 0.5
    X_SCALE = 1.0 / float(D) ** 0.5
    assert D == P and T % E == 0 and HG * 32 == P

    with ExitStack() as ctx:
        def sb(name, shape, dt=F32):
            return ctx.enter_context(nc.sbuf_tensor(name, shape, dt))

        def sem(name):
            return ctx.enter_context(nc.semaphore(name))

        strip_dram = nc.dram_tensor("strip_scratch", [H, STRIP], F32, kind="Internal").ap()
        stack_dram = nc.dram_tensor("stack_scratch", [B, 2, H, SLOTS, HD, N], BF16, kind="Internal").ap()

        bank = ctx.enter_context(nc.psum_tensor("bank", [P, 8, 512], F32))

        ident = sb("ident", [P, P])
        res = sb("res", [P, T, D])
        norm = sb("norm", [P, T, D])
        flat = sb("flat", [P, T, D])
        featA = sb("featA", [P, B, N])
        featB = sb("featB", [P, B, N])
        xat = sb("xat", [P, B, N])
        stats = sb("stats", [P, QT, 6])
        mv = sb("mv", [P, T, 2])
        rstd = sb("rstd", [P, T])
        mhalf = sb("mhalf", [P, QT])
        parts = sb("parts", [P, B, 2, 3, N], BF16)
        q_stack = sb("q_stack", [P, H // 2, N], BF16)
        k_stack = sb("k_stack", [P, H // 2, N], BF16)
        gate = sb("gate", [P, H, N])
        zbuf = sb("zbuf", [P, 4, N])
        probT = sb("probT", [P, 2 * HG, N])
        v_all = sb("v_all", [P, B, QT, H, VW])
        v_cur = sb("v_cur", [P, QT, H, VW])
        rowmax = sb("rowmax", [P, 4])
        o_sb = sb("o_sb", [P, 2, P])
        ctx_sum = sb("ctx_sum", [P, T, H, VW])
        ctx_rec = sb("ctx_rec", [P, T, H])
        wq = sb("wq", [P, D])
        wk = sb("wk", [P, D])
        wv = sb("wv", [P, D])
        wo = sb("wo", [P, D])
        raw_w = sb("raw_w", [P, 6, D])
        wT = sb("wT", [P, 6, D])
        XWK, XWV, XWQ, XWO, FAW, FNW = range(6)
        vecs = sb("vecs", [VEC_ROWS, P])
        vecT = sb("vecT", [P, VEC_ROWS])
        bo_b = sb("bo_b", [P, D])
        bv_b = sb("bv_b", [P, D])
        xbo_b = sb("xbo_b", [P, D])
        nb_b = sb("nb_b", [P, D])
        ctx_in = sb("ctx_in", [CL, B, D])
        ctxT = sb("ctxT", [P, B, CL])
        kpT = sb("kpT", [P, B, CL])
        vp = sb("vp", [CL, B, D])
        xmax = sb("xmax", [P, T])
        xsum = sb("xsum", [P, T])
        xrec = sb("xrec", [P, T])
        w1 = sb("w1", [P, E, FF])
        hw = sb("hw", [H, 8])
        dist = sb("dist", [H, N])
        strip = sb("strip", [H, STRIP])
        w2 = parts[:, :, :, :, :].rearrange("p b k r n -> p (b k r n)").bitcast(F32)[:, 0:E * FC * D].rearrange(
            "p (e c d) -> p e c d", e=E, c=FC)
        hid = gate[:, 0:4, :].rearrange("p a (c n) -> p (a c) n", c=2)
        eo = gate[:, 4:5, :].rearrange("p a (c n) -> p (a c) n", c=2)
        pre = gate[:, 5:6, :].rearrange("p a (c n) -> p (a c) n", c=2)
        act_out = gate[:, 6:7, :].rearrange("p a (c n) -> p (a c) n", c=2)
        y_out = gate[:, 7:8, :].rearrange("p a (c n) -> p (a c) n", c=2)

        ld_x = [sem(f"ld_x{b}") for b in range(B)]
        ld_hw, ld_proj, ld_vec, ld_raw, ld_bc, ld_ctx, ld_wo, ld_ffn = (
            sem(n) for n in ("ld_hw", "ld_proj", "ld_vec", "ld_raw", "ld_bc", "ld_ctx", "ld_wo", "ld_ffn"))
        pool_step, dve_step, act_step = sem("pool_step"), sem("dve_step"), sem("act_step")
        ident_ready, dist_ready, e_ready, strip_ready = (
            sem(n) for n in ("ident_ready", "dist_ready", "e_ready", "strip_ready"))
        negw_ready = sem("negw_ready")
        strip_written, gate_loaded = sem("strip_written"), sem("gate_loaded")
        ln_stats, ln_rstd, ln_done = sem("ln_stats"), sem("ln_rstd"), sem("ln_done")
        xnT_psum, xnT_ready = sem("xnT_psum"), sem("xnT_ready")
        qk_psum, qk_hi, qk_res, qk_mid, qk_lo = (
            sem(n) for n in ("qk_psum", "qk_hi", "qk_res", "qk_mid", "qk_lo"))
        v_psum, v_ready = sem("v_psum"), sem("v_ready")
        side_psum, side_ready = sem("side_psum"), sem("side_ready")
        biased = sem("biased")
        stack_written = sem("stack_written")
        stack_loaded = [sem(f"stack_loaded{g}") for g in range(G)]
        v_copied, o_zero = sem("v_copied"), sem("o_zero")
        score_ready, gated, shifted, turned, exped, masked, pv_done, o_copied, o_turned, ctx_saved = (
            sem(n) for n in ("score_ready", "gated", "shifted", "turned", "exped", "masked", "pv_done",
                             "o_copied", "o_turned", "ctx_saved"))
        d_psum = [sem(f"d_psum{i}") for i in range(10)]
        d_out = [sem(f"d_out{i}") for i in range(10)]
        dve_passed, pool_passed = sem("dve_passed"), sem("pool_passed")
        xmax_ready = sem("xmax_ready")
        up_psum, hid_ready, down_psum, eo_ready, next_psum, pre_ready, act_ready, y_ready = (
            sem(n) for n in ("up_psum", "hid_ready", "down_psum", "eo_ready", "next_psum", "pre_ready",
                             "act_ready", "y_ready"))
        y_stored = [sem("y_stored0"), sem("y_stored1")]

        x_v = x.rearrange("b (q p) d -> b p q d", p=P)
        out_v = out.rearrange("b (q p) d -> p (b q) d", p=P)

        def steps():
            for s in range(STEPS):
                u = s // HG
                yield s, u, u // QT, u % QT, (u // QT) * HG + s % HG

        def ln(k, b):
            return k * B + b + 1

        def wait_batch(eng, signal, b, per_batch, k):
            if isinstance(b, int) and b * per_batch + k <= 0:
                return
            eng.wait_ge(signal, b * per_batch + k)

        def hold(eng, passed):
            eng.sem_inc(passed, 1)

        block = ctx.enter_context(nc.Block())

        @block.sync
        def _(sp):
            sp.dma_start(res[:, 0:QT, :], x_v[0]).then_inc(ld_x[0], 16)
            sp.dma_start(hw[:, 0:1], L0_attn_w.rearrange("(h o) -> h o", o=1)).then_inc(ld_hw, 16)
            sp.dma_start(hw[:, 1:2], L0_attn_v.rearrange("(h o) -> h o", o=1)).then_inc(ld_hw, 16)
            for dst, src in ((wq, L0_attn_Wq), (wk, L0_attn_Wk), (wv, L0_attn_Wv)):
                sp.dma_start(dst[:, :], src).then_inc(ld_proj, 16)
            for b in range(1, B):
                sp.dma_start(res[:, b * QT:(b + 1) * QT, :], x_v[b]).then_inc(ld_x[b], 16)
            sp.dma_start(vecs[ROW_B1:ROW_B1 + E * FC, :],
                         L0_ffn_b1.rearrange("e (c p) -> (e c) p", p=P)).then_inc(ld_vec, 16)
            sp.dma_start(vecs[ROW_B2:ROW_B2 + E, :], L0_ffn_b2).then_inc(ld_vec, 16)
            for row, src in ((ROW_XBQ, L0_xattn_bq), (ROW_LN_SCALE, L0_ffn_ln_scale),
                             (ROW_LN_BIAS, L0_ffn_ln_bias), (ROW_ATTN_B, L0_ffn_attn_b)):
                sp.dma_start(vecs[row:row + 1, :], src.rearrange("(o d) -> o d", o=1)).then_inc(ld_vec, 16)
            for i, src in enumerate((L0_xattn_Wk, L0_xattn_Wv, L0_xattn_Wq, L0_xattn_Wo, L0_ffn_attn_w,
                                     L0_ffn_next_w)):
                sp.dma_start(raw_w[:, i, :], src).then_inc(ld_raw, 16)
            sp.dma_start(ctx_in[:, :, :], ctx_1024.rearrange("b s d -> s b d")).then_inc(ld_ctx, 16)
            for dst, src in ((bo_b, L0_attn_bo), (bv_b, L0_xattn_bv), (xbo_b, L0_xattn_bo),
                             (nb_b, L0_ffn_next_b)):
                sp.dma_start(dst[:, :], bass.AP(tensor=src.tensor, offset=0, ap=[[0, P], [1, D]])
                             ).then_inc(ld_bc, 16)
            sp.dma_start(wo[:, :], L0_attn_Wo).then_inc(ld_wo, 16)
            sp.wait_ge(strip_ready, 1)
            sp.dma_start(strip_dram, strip[:, :]).then_inc(strip_written, 16)
            sp.wait_ge(strip_written, 16)
            for g in range(G):
                sp.dma_start(gate[:, g * HG:(g + 1) * HG, :],
                             bass.AP(tensor=strip_dram.tensor, offset=g * HG * STRIP,
                                     ap=[[1, P], [STRIP, HG], [1, N]])).then_inc(gate_loaded, 16)
            def stack_batch(b, first):
                sp.wait_ge(qk_lo, b * 2 + 2)
                for qk, plan in ((0, Q_PART), (1, K_PART)):
                    for slot, part in enumerate(plan):
                        sp.dma_start(stack_dram[b, qk, :, slot, :, :], parts[:, b, qk, part, :]
                                     ).then_inc(stack_written, 16)
                sp.wait_ge(stack_written, b * (32 * SLOTS) + 32 * SLOTS)
                for g in range(G):
                    if not first:
                        sp.wait_ge(score_ready, b * STEPS - STEPS + (g + 1) * QT * HG)
                    for qk, dst in ((0, q_stack), (1, k_stack)):
                        for i in range(2):
                            h0 = g * HG + i
                            sp.dma_start(dst[64 * i:64 * i + SLOTS * HD, 2 * g:2 * g + 2, :],
                                         stack_dram[b, qk, h0:h0 + 3:2, :, :, :].rearrange("h s d t -> (s d) h t")
                                         ).then_inc(stack_loaded[g], 16)

            stack_batch(0, True)
            with sp.Fori(1, B) as b:
                stack_batch(b, False)
            sp.dma_start(w1[:, :, :], L0_ffn_w1.rearrange("e d f -> d e f")).then_inc(ld_ffn, 16)
            sp.dma_start(w2[:, :, :, :], L0_ffn_w2.rearrange("e (c p) d -> p e c d", p=P)).then_inc(ld_ffn, 16)
            for e in range(E):
                sp.wait_ge(y_ready, e + 1)
                sp.dma_start(out_v[:, e:T:E, :], y_out[:, e % 2, :].rearrange("p (m d) -> p m d", d=D)
                             ).then_inc(y_stored[e % 2], 16)
            for i in range(2):
                sp.wait_ge(y_stored[i], 16 * (E // 2))

        @block.gpsimd
        def _(pool):
            pool.memset(ident[:, :], 0.0).then_inc(pool_step, 1)
            pool.memset(mhalf[:, :], -0.5)
            pool.iota(dist[:, :], pattern=[[1, N]], base=0, channel_multiplier=0,
                      allow_small_or_imprecise_dtypes=True).then_inc(dist_ready, 1)
            pool.wait_ge(pool_step, 1)
            pool.affine_select(out=ident[:, :], in_=ident[:, :], compare_op=ALU.not_equal, fill=1.0, base=0,
                               pattern=[[-1, P]], channel_multiplier=1).then_inc(ident_ready, 1)
            steps_done = [1]

            def layer_norm_rstd(k, b):
                ts = slice(b * QT, (b + 1) * QT)
                pool.wait_ge(ln_stats, ln(k, b))
                pool.tensor_scalar(rstd[:, ts], mv[:, ts, 1], LN_EPS, 1.0, ALU.add, ALU.mult
                                   ).then_inc(pool_step, 1)
                steps_done[0] += 1
                pool.wait_ge(pool_step, steps_done[0])
                pool.tensor_tensor(rstd[:, ts], rstd[:, ts], mhalf[:, :], ALU.pow).then_inc(ln_rstd, 1)

            def low_part(i):
                b, qk = i // 2, i % 2
                pool.wait_ge(qk_mid, i + 1)
                pool.tensor_tensor(parts[:, b, qk, 2, :], zbuf[:, i % 4, :], parts[:, b, qk, 1, :],
                                   ALU.subtract).then_inc(qk_lo, 1)

            for b in range(B):
                layer_norm_rstd(0, b)
            for i in range(2 * B):
                low_part(i)
            pool.wait_ge(ld_bc, 64)
            for b in range(B):
                pool.wait_ge(ln_done, ln(0, b))
                for t in range(b * QT, (b + 1) * QT):
                    pool.tensor_tensor(res[:, t, :], res[:, t, :], bo_b[:, :], ALU.add).then_inc(biased, 1)

            def batch(b):
                for u in range(UNITS):
                    g, qt = u // QT, u % QT
                    if qt == 0:
                        pool.wait_ge(v_ready, b + 1)
                        wait_batch(pool, pv_done, b, UNITS, (g + 1) * QT - UNITS)
                        hs = slice(g * HG, (g + 1) * HG)
                        pool.tensor_copy(v_cur[:, :, hs, :].rearrange("p k h w -> p k (h w)"),
                                         v_all[:, b, :, hs, :].rearrange("p k h w -> p k (h w)")
                                         ).then_inc(v_copied, 1)
                    pool.wait_ge(exped, b * STEPS + HG * (u + 1))
                    hold(pool, pool_passed)
                    diag = probT[:, (u % 2) * HG:(u % 2) * HG + HG, qt * P:(qt + 1) * P]
                    pool.affine_select(out=diag, in_=diag, compare_op=ALU.is_ge, fill=0.0, base=0,
                                       pattern=[[0, HG], [1, P]], channel_multiplier=-1).then_inc(masked, 1)

            batch(0)
            with pool.Fori(1, B) as b:
                batch(b)

            for b in range(B):
                layer_norm_rstd(1, b)
            for b in range(B):
                pool.wait_ge(ln_done, ln(1, b))
                for t in range(b * QT, (b + 1) * QT):
                    pool.tensor_tensor(res[:, t, :], res[:, t, :], xbo_b[:, :], ALU.add).then_inc(biased, 1)
            for k in (2, 3):
                for b in range(B):
                    layer_norm_rstd(k, b)

        @block.scalar
        def _(act):
            def o_copy(b, u):
                if isinstance(b, int) and b * UNITS + u < 0:
                    return
                wait_batch(act, pv_done, b, UNITS, u + 1)
                wait_batch(act, o_turned, b, UNITS, u - 1)
                nc.scalar.copy(o_sb[:, u % 2, :], bank[:, 6, 0:P]).then_inc(o_copied, 1)

            def ctx_save(b, u):
                if isinstance(b, int) and b * UNITS + u < 0:
                    return
                tile = b * QT + u % QT if u >= 0 else b * QT - 1
                g = u % UNITS // QT
                wait_batch(act, o_turned, b, UNITS, u + 1)
                nc.scalar.copy(ctx_sum[:, tile, g * HG:(g + 1) * HG, :],
                               bank[:, 7, 0:P].rearrange("p (h w) -> p h w", w=32)[:, :, 0:VW]
                               ).then_inc(ctx_saved, 1)

            act.wait_ge(ld_hw, 32)
            nc.scalar.activation(hw[:, 3:4], hw[:, 1:2], ACT.Exp)
            act.wait_ge(negw_ready, 1)
            act.wait_ge(dist_ready, 1)
            nc.scalar.activation(dist[:, :], dist[:, :], ACT.Exp, bias=hw[:, 1:2], scale=hw[:, 2:3]
                                 ).then_inc(e_ready, 1)

            def high_and_mid(i):
                b, qk = i // 2, i % 2
                act.wait_ge(qk_psum, i + 1)
                nc.scalar.copy(parts[:, b, qk, 0, :], bank[:, 2 + i % 4, :]).then_inc(qk_hi, 1)

            def mid(i):
                b, qk = i // 2, i % 2
                act.wait_ge(qk_res, i + 1)
                nc.scalar.copy(parts[:, b, qk, 1, :], zbuf[:, i % 4, :]).then_inc(qk_mid, 1)

            for b in range(B):
                act.wait_ge(xnT_psum, b + 1)
                nc.scalar.copy(featA[:, b, :], bank[:, b % 2, :]).then_inc(xnT_ready, 1)
                high_and_mid(2 * b)
                high_and_mid(2 * b + 1)
                mid(2 * b)
                mid(2 * b + 1)
            act.wait_ge(side_psum, 1)
            nc.scalar.copy(vecT[:, :], bank[:, 0, 0:VEC_ROWS]).then_inc(side_ready, 1)
            act.wait_ge(side_psum, 2)
            nc.scalar.copy(wT[:, 0:4, :].rearrange("p a d -> p (a d)"), bank[:, 1, :]).then_inc(side_ready, 1)
            act.wait_ge(side_psum, 3)
            nc.scalar.copy(wT[:, 4:6, :].rearrange("p a d -> p (a d)"), bank[:, 2, 0:2 * D]
                           ).then_inc(side_ready, 1)
            act.wait_ge(side_psum, 4)
            nc.scalar.copy(ctxT[:, :, :].rearrange("p b s -> p (b s)"), bank[:, 3, 0:B * CL]
                           ).then_inc(side_ready, 1)
            act.wait_ge(side_psum, 5)
            nc.scalar.copy(kpT[:, :, :].rearrange("p b s -> p (b s)"), bank[:, 4, 0:B * CL]
                           ).then_inc(side_ready, 1)

            def batch(b):
                for s, u, g, qt, h in steps():
                    n = (qt + 1) * P
                    act.wait_ge(turned, b * STEPS + s + 1)
                    if s % HG == 0:
                        wait_batch(act, pv_done, b, UNITS, u - 1)
                    nc.scalar.activation(probT[:, (u % 2) * HG + s % HG, 0:n], bank[:, 4 + s % 2, 0:n],
                                         ACT.Exp).then_inc(exped, 1)
                    if s % HG == 2:
                        o_copy(b, u - 1)
                    if s % HG == 3:
                        ctx_save(b, u - 1)

            batch(0)
            with act.Fori(1, B) as b:
                batch(b)
            o_copy(B, -1)
            ctx_save(B, -1)

            for b in range(B):
                act.wait_ge(d_psum[1], b + 1)
                nc.scalar.copy(featA[:, b, :], bank[:, b, :]).then_inc(d_out[1], 1)
            for b in range(B):
                act.wait_ge(d_psum[3], b + 1)
                nc.scalar.copy(featA[:, b, :], bank[:, b, :]).then_inc(d_out[3], 1)
            for b in range(B):
                act.wait_ge(d_psum[4], b + 1)
                nc.scalar.activation(featB[:, b, :], bank[:, 4 + b, :], ACT.Identity,
                                     bias=vecT[:, ROW_XBQ:ROW_XBQ + 1]).then_inc(d_out[4], 1)
            for b in range(B):
                act.wait_ge(xmax_ready, b + 1)
                for q in range(QT):
                    t = b * QT + q
                    last = nc.scalar.activation(probT[:, HG + b, q * P:q * P + CL], bank[:, b, q * P:q * P + CL],
                                                ACT.Exp, bias=xmax[:, t:t + 1], scale=X_SCALE,
                                                accum_out=xsum[:, t:t + 1])
                last.then_inc(d_out[5], 1)
            for b in range(B):
                act.wait_ge(d_psum[7], b + 1)
                nc.scalar.copy(featA[:, b, :], bank[:, b, :]).then_inc(d_out[7], 1)
            for b in range(B):
                act.wait_ge(d_psum[8], b + 1)
                nc.scalar.activation(featB[:, b, :], bank[:, b, :], ACT.Identity,
                                     bias=vecT[:, ROW_LN_BIAS:ROW_LN_BIAS + 1],
                                     scale=vecT[:, ROW_LN_SCALE:ROW_LN_SCALE + 1]).then_inc(d_out[8], 1)
            for b in range(B):
                act.wait_ge(d_psum[9], b + 1)
                nc.scalar.activation(xat[:, b, :], bank[:, 4 + b, :], ACT.Identity,
                                     bias=vecT[:, ROW_ATTN_B:ROW_ATTN_B + 1]).then_inc(d_out[9], 1)
            for e in range(E + 2):
                if e < E:
                    for c in range(FC):
                        act.wait_ge(up_psum, e * FC + c // 2 * 2 + 2)
                        if e >= 2 and c == 0:
                            act.wait_ge(down_psum, e - 1)
                        nc.scalar.activation(hid[:, (e % 2) * FC + c, :],
                                             bank[:, 2 * (e % 2) + c // 2, (c % 2) * 256:(c % 2) * 256 + 256],
                                             ACT.Gelu, bias=vecT[:, ROW_B1 + e * FC + c:ROW_B1 + e * FC + c + 1]
                                             ).then_inc(hid_ready, 1)
                if e >= 2:
                    act.wait_ge(pre_ready, e - 1)
                    if e >= 4:
                        act.wait_ge(y_ready, e - 3)
                    nc.scalar.activation(act_out[:, e % 2, :], pre[:, e % 2, :], ACT.Gelu).then_inc(act_ready, 1)

        @block.vector
        def _(dve):
            chain = [0]

            def link(ins):
                chain[0] += 1
                ins.then_inc(dve_step, 1)
                dve.wait_ge(dve_step, chain[0])

            def layer_norm_stats(k, b):
                for q in range(QT):
                    last = dve.bn_stats(stats[:, q, :], res[:, b * QT + q, :] if k < 3 else flat[:, b * QT + q, :])
                link(last)
                for q in range(QT):
                    last = dve.bn_aggr(mv[:, b * QT + q, :], stats[:, q, :])
                last.then_inc(ln_stats, 1)
                dve.wait_ge(ln_stats, ln(k, b))

            def layer_norm_apply(k, b):
                src, dst = (res, norm) if k < 2 else (res, flat) if k == 2 else (flat, norm)
                dve.wait_ge(ln_rstd, ln(k, b))
                for q in range(QT):
                    t = b * QT + q
                    last = dve.tensor_scalar(dst[:, t, :], src[:, t, :], mv[:, t, 0:1], rstd[:, t:t + 1],
                                             ALU.subtract, ALU.mult)
                last.then_inc(ln_done, 1)

            dve.memset(strip[:, 0:P - 1], 0.0)
            dve.memset(strip[:, STRIP - 1:STRIP], 0.0)
            dve.memset(v_all[:, :, :, :, HD:VW].rearrange("p b k h w -> p (b k h w)"), 1.0)
            dve.memset(bank[:, 6, 0:P], 0.0).then_inc(o_zero, 1)
            dve.wait_ge(ld_hw, 32)
            dve.tensor_scalar(hw[:, 2:3], hw[:, 0:1], -1.0, None, ALU.mult).then_inc(negw_ready, 1)
            dve.wait_ge(ld_x[0], 16)
            layer_norm_stats(0, 0)
            for b in range(B):
                if b + 1 < B:
                    dve.wait_ge(ld_x[b + 1], 16)
                    layer_norm_stats(0, b + 1)
                layer_norm_apply(0, b)
                if b == 0:
                    dve.wait_ge(e_ready, 1)
                    link(dve.tensor_scalar(hw[:, 4:5], hw[:, 3:4], 1.0, SCORE_SCALE, ALU.add, ALU.mult))
                    link(dve.tensor_scalar(dist[:, :], dist[:, :], 1.0, None, ALU.add))
                    link(dve.reciprocal(dist[:, :], dist[:, :]))
                    dve.tensor_scalar(strip[:, P - 1:P - 1 + N], dist[:, :], hw[:, 4:5], None, ALU.mult
                                      ).then_inc(strip_ready, 1)
            for b in range(B):
                for qk in range(2):
                    i = 2 * b + qk
                    dve.wait_ge(qk_hi, i + 1)
                    if i >= 4:
                        dve.wait_ge(qk_lo, i - 3)
                    dve.tensor_tensor(zbuf[:, i % 4, :], bank[:, 2 + i % 4, :], parts[:, b, qk, 0, :],
                                      ALU.subtract).then_inc(qk_res, 1)
                dve.wait_ge(v_psum, b + 1)
                dve.tensor_copy(v_all[:, b, :, :, 0:HD].rearrange("p k h w -> p (k h) w"),
                                bank[:, 7, :].rearrange("p (k h w) -> p (k h) w", h=H, w=HD)
                                ).then_inc(v_ready, 1)
            dve.wait_ge(side_psum, 6)
            dve.wait_ge(ld_bc, 64)
            dve.tensor_tensor(vp[:, :, :], bank[0:CL, 5, :].rearrange("p (b d) -> p b d", d=D),
                              bv_b[0:CL, :].rearrange("p (o d) -> p o d", o=1).to_broadcast([CL, B, D]),
                              ALU.add).then_inc(side_ready, 1)
            dve.wait_ge(qk_lo, 2 * B)

            dve.wait_ge(gate_loaded, 16 * G)
            def shift(b, s):
                if isinstance(b, int) and b * STEPS + s < 0:
                    return
                n = (s // HG % QT + 1) * P
                wait_batch(dve, gated, b, STEPS, s + 1)
                dve.tensor_scalar(zbuf[:, s % 4, 0:n], zbuf[:, s % 4, 0:n], 0.0, rowmax[:, s % 4:s % 4 + 1],
                                  ALU.max, ALU.subtract).then_inc(shifted, 1)

            def batch(b):
                for s, u, g, qt, h in steps():
                    n = (qt + 1) * P
                    wait_batch(dve, turned, b, STEPS, s - 3)
                    dve.wait_ge(score_ready, b * STEPS + s + 1)
                    hold(dve, dve_passed)
                    dve.tensor_tensor_reduce(zbuf[:, s % 4, 0:n], bank[:, s % 4, 0:n],
                                             gate[:, h, 0:n][:, ::-1], 1.0, 0.0, ALU.mult, ALU.max,
                                             rowmax[:, s % 4:s % 4 + 1]).then_inc(gated, 1)
                    shift(b, s - 1)

            batch(0)
            with dve.Fori(1, B) as b:
                batch(b)
            shift(B, -1)

            dve.wait_ge(ctx_saved, B * UNITS)
            link(dve.reciprocal(ctx_rec[:, :, :], ctx_sum[:, :, :, HD]))
            for b in range(B):
                ts = slice(b * QT, (b + 1) * QT)
                dve.tensor_tensor(norm[:, ts, :].rearrange("p t (h w) -> p (t h) w", w=HD),
                                  ctx_sum[:, ts, :, 0:HD].rearrange("p t h w -> p (t h) w"),
                                  ctx_rec[:, ts, :].rearrange("p t (h o) -> p (t h) o", o=1
                                                              ).to_broadcast([P, QT * H, HD]),
                                  ALU.mult).then_inc(d_out[0], 1)
            for b in range(B):
                ts = slice(b * QT, (b + 1) * QT)
                dve.wait_ge(d_psum[2], b + 1)
                dve.wait_ge(biased, T)
                link(dve.tensor_tensor(res[:, ts, :], bank[:, 4 + b, :].rearrange("p (t d) -> p t d", d=D),
                                       res[:, ts, :], ALU.add))
                layer_norm_stats(1, b)
            for b in range(B):
                layer_norm_apply(1, b)
            for b in range(B):
                ts = slice(b * QT, (b + 1) * QT)
                dve.wait_ge(d_psum[5], b + 1)
                link(dve.tensor_reduce(xmax[:, ts], bank[:, b, :].rearrange("p (t k) -> p t k", k=P)[:, :, 0:CL],
                                       AX.X, ALU.max))
                dve.tensor_scalar(xmax[:, ts], xmax[:, ts], -X_SCALE, None, ALU.mult).then_inc(xmax_ready, 1)
            for b in range(B):
                dve.wait_ge(d_psum[6], b + 1)
                dve.tensor_copy(probT[0:CL, b, :], bank[0:CL, 4 + b, :]).then_inc(d_out[6], 1)
            dve.wait_ge(d_out[5], B)
            link(dve.reciprocal(xrec[:, :], xsum[:, :]))
            dve.wait_ge(biased, 2 * T)
            for b in range(B):
                dve.wait_ge(d_out[2], b + 1)
                for q in range(QT):
                    t = b * QT + q
                    last = dve.scalar_tensor_tensor(out=res[:, t, :], in0=bank[:, 4 + b, q * P:(q + 1) * P],
                                                    scalar=xrec[:, t:t + 1], in1=res[:, t, :],
                                                    op0=ALU.mult, op1=ALU.add)
                link(last)
                layer_norm_stats(2, b)
            for b in range(B):
                layer_norm_apply(2, b)
                dve.wait_ge(ln_done, ln(2, b))
                layer_norm_stats(3, b)
            for b in range(B):
                layer_norm_apply(3, b)

            for e in range(E + 2):
                if e >= 1 and e - 1 < E:
                    f = e - 1
                    dve.wait_ge(down_psum, f + 1)
                    if f >= 2:
                        dve.wait_ge(next_psum, f - 1)
                    dve.tensor_scalar(eo[:, f % 2, :], bank[:, 4 + f % 2, 0:256],
                                      vecT[:, ROW_B2 + f:ROW_B2 + f + 1], None, ALU.add).then_inc(eo_ready, 1)
                    dve.wait_ge(next_psum, f + 1)
                    if f >= 2:
                        dve.wait_ge(act_ready, f - 1)
                    dve.tensor_tensor(pre[:, f % 2, :].rearrange("p (m d) -> p m d", d=D),
                                      bank[:, 6 + f % 2, 0:256].rearrange("p (m d) -> p m d", d=D),
                                      nb_b[:, :].rearrange("p (o d) -> p o d", o=1).to_broadcast([P, MB, D]),
                                      ALU.add).then_inc(pre_ready, 1)
                if e >= 2:
                    f = e - 2
                    dve.wait_ge(act_ready, f + 1)
                    if f >= 2:
                        dve.wait_ge(y_stored[f % 2], 16 * (f // 2))
                    dve.tensor_tensor(y_out[:, f % 2, :].rearrange("p (m d) -> p m d", d=D),
                                      act_out[:, f % 2, :].rearrange("p (m d) -> p m d", d=D),
                                      res[:, f:T:E, :], ALU.add).then_inc(y_ready, 1)

        @block.tensor
        def _(pe):
            mm, turn = nc.tensor.matmul, nc.tensor.transpose
            pe.wait_ge(ident_ready, 1)
            pe.wait_ge(ld_proj, 48)
            for b in range(B):
                pe.wait_ge(ln_done, ln(0, b))
                if b >= 2:
                    pe.wait_ge(xnT_ready, b - 1)
                for q in range(QT):
                    last = turn(bank[:, b % 2, q * P:(q + 1) * P], norm[:, b * QT + q, :], ident[:, :])
                last.then_inc(xnT_psum, 1)
                pe.wait_ge(xnT_ready, b + 1)
                for i, w in ((2 * b, wq), (2 * b + 1, wk)):
                    if i >= 4:
                        pe.wait_ge(qk_res, i - 3)
                    mm(bank[:, 2 + i % 4, :], w[:, :], featA[:, b, :], start=True, stop=True).then_inc(qk_psum, 1)
                if b >= 1:
                    pe.wait_ge(v_ready, b)
                for q in range(QT):
                    last = mm(bank[:, 7, q * P:(q + 1) * P], featA[:, b, q * P:(q + 1) * P], wv[:, :],
                              start=True, stop=True)
                last.then_inc(v_psum, 1)
            pe.wait_ge(ld_vec, 96)
            pe.wait_ge(xnT_ready, B)
            turn(bank[:, 0, 0:VEC_ROWS], vecs[:, :], ident[0:VEC_ROWS, 0:VEC_ROWS]).then_inc(side_psum, 1)
            pe.wait_ge(ld_raw, 96)
            for i in range(4):
                last = turn(bank[:, 1, i * P:(i + 1) * P], raw_w[:, i, :], ident[:, :])
            last.then_inc(side_psum, 1)
            pe.wait_ge(qk_res, 2 * B)
            for i in range(2):
                last = turn(bank[:, 2, i * P:(i + 1) * P], raw_w[:, 4 + i, :], ident[:, :])
            last.then_inc(side_psum, 1)
            pe.wait_ge(ld_ctx, 16)
            for b in range(B):
                last = turn(bank[:, 3, b * CL:(b + 1) * CL], ctx_in[:, b, :], ident[0:CL, 0:CL])
            last.then_inc(side_psum, 1)
            pe.wait_ge(side_ready, 4)
            mm(bank[:, 4, 0:B * CL], wT[:, XWK, :], ctxT[:, :, :].rearrange("p b s -> p (b s)"),
               start=True, stop=True).then_inc(side_psum, 1)
            for b in range(B):
                last = mm(bank[0:CL, 5, b * P:(b + 1) * P], ctxT[:, b, :], wT[:, XWV, :], start=True, stop=True)
            last.then_inc(side_psum, 1)
            pe.wait_ge(side_ready, 6)
            pe.wait_ge(v_ready, B)
            pe.wait_ge(o_zero, 1)

            plan = list(steps())

            def scores(b, s):
                _, u, g, qt, h = plan[s]
                n, i, j = (qt + 1) * P, h % 2, h // 2
                if s % (QT * HG) == 0:
                    pe.wait_ge(stack_loaded[g], b * 64 + 64)
                wait_batch(pe, gated, b, STEPS, s - 3)
                r = slice(64 * i, 64 * i + SLOTS * HD)
                mm(bank[:, s % 4, 0:n], q_stack[r, j, qt * P:(qt + 1) * P], k_stack[r, j, 0:n],
                   start=True, stop=True).then_inc(score_ready, 1)

            def turn_step(b, s):
                if isinstance(b, int) and b * STEPS + s < 0:
                    return
                qt = s // HG % QT
                wait_batch(pe, shifted, b, STEPS, s + 1)
                wait_batch(pe, exped, b, STEPS, s - 1)
                for k in range(qt + 1):
                    last = turn(bank[:, 4 + s % 2, k * P:(k + 1) * P], zbuf[:, s % 4, k * P:(k + 1) * P],
                                ident[:, :])
                last.then_inc(turned, 1)

            def values(b, u):
                if isinstance(b, int) and b * UNITS + u < 0:
                    return
                g, qt = u % UNITS // QT, u % QT
                wait_batch(pe, masked, b, UNITS, u + 1)
                wait_batch(pe, o_copied, b, UNITS, u)
                if qt == 0:
                    wait_batch(pe, v_copied, b, G, g + 1)
                for k in range(qt + 1):
                    for i in range(HG):
                        last = mm(bank[32 * i:32 * i + VW, 6, 0:P], v_cur[:, k, g * HG + i, :],
                                  probT[:, (u % 2) * HG + i, k * P:(k + 1) * P],
                                  start=(k == 0), stop=(k == qt))
                last.then_inc(pv_done, 1)

            def turn_context(b, u):
                if isinstance(b, int) and b * UNITS + u < 0:
                    return
                wait_batch(pe, o_copied, b, UNITS, u + 1)
                wait_batch(pe, ctx_saved, b, UNITS, u)
                turn(bank[:, 7, 0:P], o_sb[:, u % 2, :], ident[:, :]).then_inc(o_turned, 1)

            def batch(b, last_batch):
                for s in range(STEPS):
                    if s + 3 < STEPS:
                        scores(b, s + 3)
                    elif not last_batch:
                        scores(b + 1, s + 3 - STEPS)
                    turn_step(b, s - 1)
                    if s % HG == 3:
                        values(b, s // HG - 1)
                    if s % HG == 0:
                        turn_context(b, s // HG - 2)

            for s in range(3):
                scores(0, s)
            batch(0, False)
            with pe.Fori(1, B - 1) as b:
                batch(b, False)
            batch(B - 1, True)
            turn_step(B, -1)
            turn_context(B, -2)
            values(B, -1)
            turn_context(B, -1)

            for b in range(B):
                pe.wait_ge(d_out[0], b + 1)
                for q in range(QT):
                    last = turn(bank[:, b, q * P:(q + 1) * P], norm[:, b * QT + q, :], ident[:, :])
                last.then_inc(d_psum[1], 1)
            pe.wait_ge(ld_wo, 16)
            for b in range(B):
                pe.wait_ge(d_out[1], b + 1)
                for q in range(QT):
                    last = mm(bank[:, 4 + b, q * P:(q + 1) * P], featA[:, b, q * P:(q + 1) * P], wo[:, :],
                              start=True, stop=True)
                last.then_inc(d_psum[2], 1)
            for b in range(B):
                pe.wait_ge(ln_done, ln(1, b))
                for q in range(QT):
                    last = turn(bank[:, b, q * P:(q + 1) * P], norm[:, b * QT + q, :], ident[:, :])
                last.then_inc(d_psum[3], 1)
            for b in range(B):
                pe.wait_ge(d_out[3], b + 1)
                mm(bank[:, 4 + b, :], wT[:, XWQ, :], featA[:, b, :], start=True, stop=True).then_inc(d_psum[4], 1)
            for b in range(B):
                pe.wait_ge(d_out[4], b + 1)
                for q in range(QT):
                    last = mm(bank[:, b, q * P:q * P + CL], featB[:, b, q * P:(q + 1) * P], kpT[:, b, :],
                              start=True, stop=True)
                last.then_inc(d_psum[5], 1)
            for b in range(B):
                pe.wait_ge(d_out[5], b + 1)
                for q in range(QT):
                    last = turn(bank[0:CL, 4 + b, q * P:(q + 1) * P], probT[:, HG + b, q * P:q * P + CL],
                                ident[:, :])
                last.then_inc(d_psum[6], 1)
            for b in range(B):
                pe.wait_ge(d_out[6], b + 1)
                mm(bank[:, b, :], vp[:, b, :], probT[0:CL, b, :], start=True, stop=True).then_inc(d_psum[7], 1)
            for b in range(B):
                pe.wait_ge(d_out[7], b + 1)
                for q in range(QT):
                    last = mm(bank[:, 4 + b, q * P:(q + 1) * P], featA[:, b, q * P:(q + 1) * P], wT[:, XWO, :],
                              start=True, stop=True)
                last.then_inc(d_out[2], 1)
            for b in range(B):
                pe.wait_ge(ln_done, ln(3, b))
                for q in range(QT):
                    last = turn(bank[:, b, q * P:(q + 1) * P], norm[:, b * QT + q, :], ident[:, :])
                last.then_inc(d_psum[8], 1)
            for b in range(B):
                pe.wait_ge(d_out[8], b + 1)
                mm(bank[:, 4 + b, :], wT[:, FAW, :], featB[:, b, :], start=True, stop=False,
                   skip_group_check=True)
                for q in range(QT):
                    last = mm(bank[:, 4 + b, q * P:(q + 1) * P], flat[:, b * QT + q, :], ident[:, :],
                              start=False, stop=(q == QT - 1), skip_group_check=True)
                last.then_inc(d_psum[9], 1)
            pe.wait_ge(ld_ffn, 32)
            pe.wait_ge(d_out[9], B)
            xat_v = xat[:, :, :].rearrange("p b n -> p (b n)").rearrange("p (m e n) -> p e m n", m=MB, n=P)
            for e in range(E + 2):
                if e < E:
                    for c in range(FC):
                        if e >= 2 and c % 2 == 0:
                            pe.wait_ge(hid_ready, (e - 2) * FC + c + 2)
                        mm(bank[:, 2 * (e % 2) + c // 2, (c % 2) * 256:(c % 2) * 256 + 256],
                           w1[:, e, c * P:(c + 1) * P], xat_v[:, e], start=True, stop=True).then_inc(up_psum, 1)
                if e >= 1 and e - 1 < E:
                    f = e - 1
                    if f >= 2:
                        pe.wait_ge(eo_ready, f - 1)
                    for c in range(FC):
                        pe.wait_ge(hid_ready, f * FC + c + 1)
                        last = mm(bank[:, 4 + f % 2, 0:256], w2[:, f, c, :], hid[:, (f % 2) * FC + c, :],
                                  start=(c == 0), stop=(c == FC - 1))
                    last.then_inc(down_psum, 1)
                    pe.wait_ge(eo_ready, f + 1)
                    if f >= 2:
                        pe.wait_ge(pre_ready, f - 1)
                    for m in range(MB):
                        last = mm(bank[:, 6 + f % 2, m * P:(m + 1) * P], eo[:, f % 2, m * P:(m + 1) * P],
                                  wT[:, FNW, :], start=True, stop=True)
                    last.then_inc(next_psum, 1)


_INS = ['x', 'ctx_1024', 'L0_attn_Wq', 'L0_attn_Wk', 'L0_attn_Wv', 'L0_attn_Wo', 'L0_attn_bo', 'L0_attn_w',
        'L0_attn_v', 'L0_xattn_Wk', 'L0_xattn_Wv', 'L0_xattn_bv', 'L0_xattn_Wq', 'L0_xattn_bq', 'L0_xattn_Wo',
        'L0_xattn_bo', 'L0_ffn_ln_scale', 'L0_ffn_ln_bias', 'L0_ffn_attn_w', 'L0_ffn_attn_b', 'L0_ffn_w1',
        'L0_ffn_b1', 'L0_ffn_w2', 'L0_ffn_b2', 'L0_ffn_next_w', 'L0_ffn_next_b']


def kernel(**inputs):
    import numpy as _np
    import concourse.bacc as _bacc
    from concourse import mybir as _mybir
    from concourse.bass_utils import run_bass_kernel_spmd as _run

    nc = _bacc.Bacc("TRN2", target_bir_lowering=False, num_devices=1)
    arrays, args = {}, []
    for name in _INS:
        a = _np.ascontiguousarray(inputs[name])
        arrays[f"in_{name}"] = a
        args.append(nc.dram_tensor(f"in_{name}", a.shape, _mybir.dt.from_np(a.dtype), kind="ExternalInput").ap())
    shape = tuple(inputs["x"].shape)
    args.append(nc.dram_tensor("out_x", shape, _mybir.dt.float32, kind="ExternalOutput").ap())
    decoder_kernel(nc, *args)
    r = _run(nc, [arrays], core_ids=[0])
    return r.results[0]["out_x"]
```

```python
from contextlib import ExitStack

import concourse.bass as bass
from concourse import mybir

ALU = mybir.AluOpType
ACT = mybir.ActivationFunctionType
AX = mybir.AxisListType
F32 = mybir.dt.float32
BF16 = mybir.dt.bfloat16

P = 128
LN_EPS = 1e-5
Q_PART = (0, 0, 1, 0, 2, 1)
K_PART = (0, 1, 0, 2, 0, 1)
SLOTS = len(Q_PART)
ROW_B1, ROW_B2, ROW_XBQ, ROW_LN_SCALE, ROW_LN_BIAS, ROW_ATTN_B, VEC_ROWS = 0, 32, 40, 41, 42, 43, 44


def decoder_kernel(nc, x, ctx_1024, L0_attn_Wq, L0_attn_Wk, L0_attn_Wv, L0_attn_Wo, L0_attn_bo, L0_attn_w,
                   L0_attn_v, L0_xattn_Wk, L0_xattn_Wv, L0_xattn_bv, L0_xattn_Wq, L0_xattn_bq, L0_xattn_Wo,
                   L0_xattn_bo, L0_ffn_ln_scale, L0_ffn_ln_bias, L0_ffn_attn_w, L0_ffn_attn_b, L0_ffn_w1,
                   L0_ffn_b1, L0_ffn_w2, L0_ffn_b2, L0_ffn_next_w, L0_ffn_next_b, out):
    B, N, D = x.shape
    H = L0_attn_w.shape[0]
    HD = D // H
    CL = ctx_1024.shape[1]
    E, _, FF = L0_ffn_w1.shape
    QT = N // P
    T = B * QT
    FC = FF // P
    HG = 4
    G = H // HG
    UNITS = G * QT
    STEPS = UNITS * HG
    VW = HD + 1
    MB = T // E
    STRIP = N + P
    PAIRS = E // QT
    BATCH_OF = [m * PAIRS + p for p in range(PAIRS) for m in range(MB)]
    ZS = 8
    SCORE_SCALE = 1.0 / float(HD) ** 0.5
    X_SCALE = 1.0 / float(D) ** 0.5
    assert D == P and T % E == 0 and HG * 32 == P and PAIRS * MB == B and MB == 2

    with ExitStack() as ctx:
        def sb(name, shape, dt=F32):
            return ctx.enter_context(nc.sbuf_tensor(name, shape, dt))

        def sem(name):
            return ctx.enter_context(nc.semaphore(name))

        strip_dram = nc.dram_tensor("strip_scratch", [H, STRIP], F32, kind="Internal").ap()
        stack_dram = nc.dram_tensor("stack_scratch", [B, 2, H, SLOTS, HD, N], BF16, kind="Internal").ap()

        bank = ctx.enter_context(nc.psum_tensor("bank", [P, 8, 512], F32))

        ident = sb("ident", [P, P])
        res = sb("res", [P, T, D])
        norm = sb("norm", [P, T, D])
        flat = sb("flat", [P, T, D])
        featA = sb("featA", [P, B, N])
        featB = sb("featB", [P, B, N])
        xat = sb("xat", [P, B, N])
        stats = sb("stats", [P, QT, 6])
        mv = sb("mv", [P, T, 2])
        rstd = sb("rstd", [P, T])
        mhalf = sb("mhalf", [P, QT])
        parts = sb("parts", [P, B, 2, 3, N], BF16)
        q_stack = sb("q_stack", [P, H // 2, N], BF16)
        k_stack = sb("k_stack", [P, H // 2, N], BF16)
        gate = sb("gate", [P, H, N])
        zbuf = sb("zbuf", [P, ZS, N])
        probT = sb("probT", [P, 2 * HG, N])
        v_all = sb("v_all", [P, B, QT, H, VW])
        v_cur = sb("v_cur", [P, QT, H, VW])
        rowmax = sb("rowmax", [P, ZS])
        o_sb = sb("o_sb", [P, 2, P])
        ctx_sum = sb("ctx_sum", [P, T, H, VW])
        ctx_rec = sb("ctx_rec", [P, T, H])
        wq = sb("wq", [P, D])
        wk = sb("wk", [P, D])
        wv = sb("wv", [P, D])
        wo = sb("wo", [P, D])
        wT = sb("wT", [P, 6, D])
        XWK, XWV, XWQ, XWO, FAW, FNW = range(6)
        vecs = sb("vecs", [VEC_ROWS, P])
        vecT = sb("vecT", [P, VEC_ROWS])
        bo_b = sb("bo_b", [P, D])
        bv_b = sb("bv_b", [P, D])
        xbo_b = sb("xbo_b", [P, D])
        nb_b = sb("nb_b", [P, D])
        ctx_in = sb("ctx_in", [CL, B, D])
        ctxT = sb("ctxT", [P, B, CL])
        kpT = sb("kpT", [P, B, CL])
        vp = sb("vp", [CL, B, D])
        xmax = sb("xmax", [P, T])
        xsum = sb("xsum", [P, T])
        xrec = sb("xrec", [P, T])
        w1 = sb("w1", [P, E, FF])
        hw = sb("hw", [H, 8])
        raw_w = flat[:, 0:6, :]
        dist = xat[0:H, 0, :]
        strip = xat[0:H, 1:3, :].rearrange("h a n -> h (a n)")[:, 0:STRIP]
        xprob = probT[:, HG:2 * HG, :]
        xprobT = probT[0:CL, 0:HG, :]
        w2 = parts[:, :, :, :, :].rearrange("p b k r n -> p (b k r n)").bitcast(F32)[:, 0:E * FC * D].rearrange(
            "p (e c d) -> p e c d", e=E, c=FC)
        hid = gate[:, 0:4, :].rearrange("p a (c n) -> p (a c) n", c=2)
        eo = gate[:, 4:5, :].rearrange("p a (c n) -> p (a c) n", c=2)
        pre = gate[:, 5:6, :].rearrange("p a (c n) -> p (a c) n", c=2)
        act_out = gate[:, 6:7, :].rearrange("p a (c n) -> p (a c) n", c=2)
        y_out = gate[:, 7:8, :].rearrange("p a (c n) -> p (a c) n", c=2)

        ld_x = [sem(f"ld_x{b}") for b in range(B)]
        ld_hw, ld_proj, ld_vec, ld_raw, ld_bc, ld_ctx, ld_wo, ld_ffn = (
            sem(n) for n in ("ld_hw", "ld_proj", "ld_vec", "ld_raw", "ld_bc", "ld_ctx", "ld_wo", "ld_ffn"))
        pool_step, dve_step, act_step = sem("pool_step"), sem("dve_step"), sem("act_step")
        ident_ready, dist_ready, e_ready, strip_ready = (
            sem(n) for n in ("ident_ready", "dist_ready", "e_ready", "strip_ready"))
        negw_ready = sem("negw_ready")
        strip_written, gate_loaded = sem("strip_written"), sem("gate_loaded")
        ln_stats, ln_rstd, ln_done = ([sem(f"{n}{k}") for k in range(4)] for n in ("ln_stats", "ln_rstd", "ln_done"))
        xnT_psum, xnT_ready = sem("xnT_psum"), sem("xnT_ready")
        qk_psum, qk_hi, qk_res, qk_mid, qk_lo = (
            sem(n) for n in ("qk_psum", "qk_hi", "qk_res", "qk_mid", "qk_lo"))
        v_psum, v_ready = sem("v_psum"), sem("v_ready")
        side_psum, side_ready = sem("side_psum"), sem("side_ready")
        biased = sem("biased")
        stack_written = sem("stack_written")
        stack_loaded = [sem(f"stack_loaded{g}") for g in range(G)]
        v_copied, o_zero = sem("v_copied"), sem("o_zero")
        AHEAD = 5
        score_ready, rectified, gated, shifted_even, shifted_odd, turned, exped, masked, pv_done, o_copied, o_turned, ctx_saved = (
            sem(n) for n in ("score_ready", "rectified", "gated", "shifted_even", "shifted_odd", "turned", "exped", "masked", "pv_done",
                             "o_copied", "o_turned", "ctx_saved"))
        d_psum = [sem(f"d_psum{i}") for i in range(11)]
        d_out = [sem(f"d_out{i}") for i in range(11)]
        dve_passed, pool_passed = sem("dve_passed"), sem("pool_passed")
        xmax_ready = sem("xmax_ready")
        up_psum, hid_ready, down_psum, eo_ready, next_psum, pre_ready, act_ready, y_ready = (
            sem(n) for n in ("up_psum", "hid_ready", "down_psum", "eo_ready", "next_psum", "pre_ready",
                             "act_ready", "y_ready"))
        y_stored = [sem("y_stored0"), sem("y_stored1")]

        x_v = x.rearrange("b (q p) d -> b p q d", p=P)
        out_v = out.rearrange("b (q p) d -> q p b d", p=P)
        res_v = res[:, :, :].rearrange("p (b q) d -> p b q d", q=QT)

        def steps():
            for s in range(STEPS):
                u = s // HG
                yield s, u, u // QT, u % QT, (u // QT) * HG + s % HG

        def wait_batch(eng, signal, b, per_batch, k):
            if isinstance(b, int) and b * per_batch + k <= 0:
                return
            eng.wait_ge(signal, b * per_batch + k)

        def hold(eng, passed):
            eng.sem_inc(passed, 1)

        def after_attention():
            for k in range(1, 11):
                yield "stage", k, range(0, MB)
            tick = 0
            for p in range(1, PAIRS):
                for k in range(1, 11):
                    yield "stage", k, range(p * MB, (p + 1) * MB)
                    if k % 2 == 0 and tick < p * QT:
                        yield "tick", tick, None
                        tick += 1
            while tick < E + 3:
                yield "tick", tick, None
                tick += 1

        block = ctx.enter_context(nc.Block())

        @block.sync
        def _(sp):
            sp.dma_start(res[:, 0:QT, :], x_v[BATCH_OF[0]]).then_inc(ld_x[0], 16)
            sp.dma_start(hw[:, 0:1], L0_attn_w.rearrange("(h o) -> h o", o=1)).then_inc(ld_hw, 16)
            sp.dma_start(hw[:, 1:2], L0_attn_v.rearrange("(h o) -> h o", o=1)).then_inc(ld_hw, 16)
            for dst, src in ((wq, L0_attn_Wq), (wk, L0_attn_Wk), (wv, L0_attn_Wv)):
                sp.dma_start(dst[:, :], src).then_inc(ld_proj, 16)
            for b in range(1, B):
                sp.dma_start(res[:, b * QT:(b + 1) * QT, :], x_v[BATCH_OF[b]]).then_inc(ld_x[b], 16)
            sp.dma_start(vecs[ROW_B1:ROW_B1 + E * FC, :],
                         L0_ffn_b1.rearrange("e (c p) -> (e c) p", p=P)).then_inc(ld_vec, 16)
            sp.dma_start(vecs[ROW_B2:ROW_B2 + E, :], L0_ffn_b2).then_inc(ld_vec, 16)
            for row, src in ((ROW_XBQ, L0_xattn_bq), (ROW_LN_SCALE, L0_ffn_ln_scale),
                             (ROW_LN_BIAS, L0_ffn_ln_bias), (ROW_ATTN_B, L0_ffn_attn_b)):
                sp.dma_start(vecs[row:row + 1, :], src.rearrange("(o d) -> o d", o=1)).then_inc(ld_vec, 16)
            for i, src in enumerate((L0_xattn_Wk, L0_xattn_Wv, L0_xattn_Wq, L0_xattn_Wo, L0_ffn_attn_w,
                                     L0_ffn_next_w)):
                sp.dma_start(raw_w[:, i, :], src).then_inc(ld_raw, 16)
            for b in range(B):
                sp.dma_start(ctx_in[:, b, :], ctx_1024[BATCH_OF[b]]).then_inc(ld_ctx, 16)
            for dst, src in ((bo_b, L0_attn_bo), (bv_b, L0_xattn_bv), (xbo_b, L0_xattn_bo),
                             (nb_b, L0_ffn_next_b)):
                sp.dma_start(dst[:, :], bass.AP(tensor=src.tensor, offset=0, ap=[[0, P], [1, D]])
                             ).then_inc(ld_bc, 16)
            sp.dma_start(wo[:, :], L0_attn_Wo).then_inc(ld_wo, 16)
            sp.wait_ge(strip_ready, 1)
            sp.dma_start(strip_dram, strip).then_inc(strip_written, 16)
            sp.wait_ge(strip_written, 16)
            for g in range(G):
                sp.dma_start(gate[:, g * HG:(g + 1) * HG, :],
                             bass.AP(tensor=strip_dram.tensor, offset=g * HG * STRIP,
                                     ap=[[1, P], [STRIP, HG], [1, N]])).then_inc(gate_loaded, 16)
            def stack_batch(b, first):
                sp.wait_ge(qk_lo, b * 2 + 2)
                for qk, plan in ((0, Q_PART), (1, K_PART)):
                    for slot, part in enumerate(plan):
                        sp.dma_start(stack_dram[b, qk, :, slot, :, :], parts[:, b, qk, part, :]
                                     ).then_inc(stack_written, 16)
                sp.wait_ge(stack_written, b * (32 * SLOTS) + 32 * SLOTS)
                for g in range(G):
                    if not first:
                        sp.wait_ge(score_ready, b * STEPS - STEPS + (g + 1) * QT * HG)
                    for qk, dst in ((0, q_stack), (1, k_stack)):
                        for i in range(2):
                            h0 = g * HG + i
                            sp.dma_start(dst[64 * i:64 * i + SLOTS * HD, 2 * g:2 * g + 2, :],
                                         stack_dram[b, qk, h0:h0 + 3:2, :, :, :].rearrange("h s d t -> (s d) h t")
                                         ).then_inc(stack_loaded[g], 16)

            stack_batch(0, True)
            with sp.Fori(1, B) as b:
                stack_batch(b, False)
            sp.dma_start(w1[:, :, :], L0_ffn_w1.rearrange("e d f -> d e f")).then_inc(ld_ffn, 16)
            sp.dma_start(w2[:, :, :, :], L0_ffn_w2.rearrange("e (c p) d -> p e c d", p=P)).then_inc(ld_ffn, 16)
            for e in range(E):
                sp.wait_ge(y_ready, e + 1)
                sp.dma_start(out_v[e % QT, :, e // QT:B:PAIRS, :], y_out[:, e % 2, :].rearrange("p (m d) -> p m d", d=D)
                             ).then_inc(y_stored[e % 2], 16)
            for i in range(2):
                sp.wait_ge(y_stored[i], 16 * (E // 2))

        @block.gpsimd
        def _(pool):
            pool.memset(ident[:, :], 0.0).then_inc(pool_step, 1)
            pool.memset(mhalf[:, :], -0.5)
            pool.iota(dist, pattern=[[1, N]], base=0, channel_multiplier=0,
                      allow_small_or_imprecise_dtypes=True).then_inc(dist_ready, 1)
            pool.wait_ge(pool_step, 1)
            pool.affine_select(out=ident[:, :], in_=ident[:, :], compare_op=ALU.not_equal, fill=1.0, base=0,
                               pattern=[[-1, P]], channel_multiplier=1).then_inc(ident_ready, 1)
            steps_done = [1]

            def layer_norm_rstd(k, b):
                ts = slice(b * QT, (b + 1) * QT)
                pool.wait_ge(ln_stats[k], b + 1)
                pool.tensor_scalar(rstd[:, ts], mv[:, ts, 1], LN_EPS, 1.0, ALU.add, ALU.mult
                                   ).then_inc(pool_step, 1)
                steps_done[0] += 1
                pool.wait_ge(pool_step, steps_done[0])
                pool.tensor_tensor(rstd[:, ts], rstd[:, ts], mhalf[:, :], ALU.pow).then_inc(ln_rstd[k], 1)

            def low_part(i):
                b, qk = i // 2, i % 2
                pool.wait_ge(qk_mid, i + 1)
                pool.tensor_tensor(parts[:, b, qk, 2, :], zbuf[:, i % 4, :], parts[:, b, qk, 1, :],
                                   ALU.subtract).then_inc(qk_lo, 1)

            for b in range(B):
                layer_norm_rstd(0, b)
            for i in range(2 * B):
                low_part(i)
            pool.wait_ge(ld_bc, 64)
            for b in range(B):
                pool.wait_ge(ln_done[0], b + 1)
                for t in range(b * QT, (b + 1) * QT):
                    pool.tensor_tensor(res[:, t, :], res[:, t, :], bo_b[:, :], ALU.add).then_inc(biased, 1)

            def mask(b, u):
                if isinstance(b, int) and b * UNITS + u < 0:
                    return
                qt = u % QT
                wait_batch(pool, exped, b, STEPS, HG * (u + 1))
                hold(pool, pool_passed)
                diag = probT[:, (u % 2) * HG:(u % 2) * HG + HG, qt * P:(qt + 1) * P]
                pool.affine_select(out=diag, in_=diag, compare_op=ALU.is_ge, fill=0.0, base=0,
                                   pattern=[[0, HG], [1, P]], channel_multiplier=-1).then_inc(masked, 1)

            def batch(b):
                for s, u, g, qt, h in steps():
                    n = (qt + 1) * P
                    if s % (QT * HG) == 0:
                        pool.wait_ge(v_ready, b + 1)
                        wait_batch(pool, pv_done, b, UNITS, (g + 1) * QT - UNITS)
                        hs = slice(g * HG, (g + 1) * HG)
                        pool.tensor_copy(v_cur[:, :, hs, :].rearrange("p k h w -> p k (h w)"),
                                         v_all[:, b, :, hs, :].rearrange("p k h w -> p k (h w)")
                                         ).then_inc(v_copied, 1)
                    if s % 2 == 1:
                        pool.wait_ge(gated, b * STEPS + s + 1)
                        hold(pool, pool_passed)
                        pool.tensor_scalar(zbuf[:, s % ZS, 0:n], zbuf[:, s % ZS, 0:n], -1.0,
                                           rowmax[:, s % ZS:s % ZS + 1], ALU.mult, ALU.add
                                           ).then_inc(shifted_odd, 1)
                    if s % HG == 1:
                        mask(b, u - 1)

            batch(0)
            with pool.Fori(1, B) as b:
                batch(b)
            mask(B, -1)

            for what, k, slots in after_attention():
                if what == "stage" and k == 2:
                    for b in slots:
                        layer_norm_rstd(1, b)
                    for b in slots:
                        pool.wait_ge(ln_done[1], b + 1)
                        for t in range(b * QT, (b + 1) * QT):
                            pool.tensor_tensor(res[:, t, :], res[:, t, :], xbo_b[:, :], ALU.add
                                               ).then_inc(biased, 1)
                if what == "stage" and k == 8:
                    for b in slots:
                        layer_norm_rstd(2, b)
                    for b in slots:
                        layer_norm_rstd(3, b)

        @block.scalar
        def _(act):
            def o_copy(b, u):
                if isinstance(b, int) and b * UNITS + u < 0:
                    return
                wait_batch(act, pv_done, b, UNITS, u + 1)
                wait_batch(act, o_turned, b, UNITS, u - 1)
                nc.scalar.copy(o_sb[:, u % 2, :], bank[:, 6, 0:P]).then_inc(o_copied, 1)

            def ctx_save(b, u):
                if isinstance(b, int) and b * UNITS + u < 0:
                    return
                tile = b * QT + u % QT if u >= 0 else b * QT - QT + u % QT
                g = u % UNITS // QT
                wait_batch(act, o_turned, b, UNITS, u + 1)
                nc.scalar.copy(ctx_sum[:, tile, g * HG:(g + 1) * HG, :],
                               bank[:, 7, 0:P].rearrange("p (h w) -> p h w", w=32)[:, :, 0:VW]
                               ).then_inc(ctx_saved, 1)

            act.wait_ge(ld_hw, 32)
            nc.scalar.activation(hw[:, 3:4], hw[:, 1:2], ACT.Exp)
            act.wait_ge(negw_ready, 1)
            act.wait_ge(dist_ready, 1)
            nc.scalar.activation(dist, dist, ACT.Exp, bias=hw[:, 1:2], scale=hw[:, 2:3]
                                 ).then_inc(e_ready, 1)

            def high_and_mid(i):
                b, qk = i // 2, i % 2
                act.wait_ge(qk_psum, i + 1)
                nc.scalar.copy(parts[:, b, qk, 0, :], bank[:, 2 + i % 4, :]).then_inc(qk_hi, 1)

            def mid(i):
                b, qk = i // 2, i % 2
                act.wait_ge(qk_res, i + 1)
                nc.scalar.copy(parts[:, b, qk, 1, :], zbuf[:, i % 4, :]).then_inc(qk_mid, 1)

            for b in range(B):
                act.wait_ge(xnT_psum, b + 1)
                nc.scalar.copy(featA[:, b, :], bank[:, b % 2, :]).then_inc(xnT_ready, 1)
                high_and_mid(2 * b)
                high_and_mid(2 * b + 1)
                mid(2 * b)
                mid(2 * b + 1)
            act.wait_ge(side_psum, 1)
            nc.scalar.copy(vecT[:, :], bank[:, 0, 0:VEC_ROWS]).then_inc(side_ready, 1)
            act.wait_ge(side_psum, 2)
            nc.scalar.copy(wT[:, 0:4, :].rearrange("p a d -> p (a d)"), bank[:, 1, :]).then_inc(side_ready, 1)
            act.wait_ge(side_psum, 3)
            nc.scalar.copy(wT[:, 4:6, :].rearrange("p a d -> p (a d)"), bank[:, 2, 0:2 * D]
                           ).then_inc(side_ready, 1)
            act.wait_ge(side_psum, 4)
            nc.scalar.copy(ctxT[:, :, :].rearrange("p b s -> p (b s)"), bank[:, 3, 0:B * CL]
                           ).then_inc(side_ready, 1)
            act.wait_ge(side_psum, 5)
            nc.scalar.copy(kpT[:, :, :].rearrange("p b s -> p (b s)"), bank[:, 4, 0:B * CL]
                           ).then_inc(side_ready, 1)

            def rectify(b, s):
                n = (s // HG % QT + 1) * P
                act.wait_ge(score_ready, b * STEPS + s + 1)
                nc.scalar.activation(bank[:, s % 4, 0:n], bank[:, s % 4, 0:n], ACT.Relu).then_inc(rectified, 1)

            def batch(b, last_batch):
                for s, u, g, qt, h in steps():
                    n = (qt + 1) * P
                    act.wait_ge(turned, b * STEPS + s + 1)
                    if s % HG == 0:
                        wait_batch(act, pv_done, b, UNITS, u - 1)
                    nc.scalar.activation(probT[:, (u % 2) * HG + s % HG, 0:n], bank[:, 4 + s % 2, 0:n],
                                         ACT.Exp, scale=-1.0 if s % 2 else 1.0).then_inc(exped, 1)
                    if s % 2 == 0:
                        if s + AHEAD < STEPS:
                            rectify(b, s + AHEAD)
                        elif not last_batch:
                            rectify(b + 1, s + AHEAD - STEPS)
                    if s % HG == 2:
                        o_copy(b, u - 1)
                    if s % HG == 0:
                        ctx_save(b, u - 2)

            for s in range(1, AHEAD, 2):
                rectify(0, s)
            batch(0, False)
            with act.Fori(1, B - 1) as b:
                batch(b, False)
            batch(B - 1, True)
            ctx_save(B, -2)
            o_copy(B, -1)
            ctx_save(B, -1)

            def stage(k, slots):
                for b in slots:
                    low, high = bank[:, b % MB, :], bank[:, MB + b % MB, :]
                    if k in (1, 3, 7):
                        act.wait_ge(d_psum[k], b + 1)
                        nc.scalar.copy(featA[:, b, :], low).then_inc(d_out[k], 1)
                    elif k == 4:
                        act.wait_ge(d_psum[4], b + 1)
                        nc.scalar.activation(featB[:, b, :], high, ACT.Identity,
                                             bias=vecT[:, ROW_XBQ:ROW_XBQ + 1]).then_inc(d_out[4], 1)
                    elif k == 5:
                        act.wait_ge(xmax_ready, b + 1)
                        for q in range(QT):
                            t = b * QT + q
                            last = nc.scalar.activation(xprob[:, b, q * P:q * P + CL], low[:, q * P:q * P + CL],
                                                        ACT.Exp, bias=xmax[:, t:t + 1], scale=X_SCALE,
                                                        accum_out=xsum[:, t:t + 1])
                        last.then_inc(d_out[5], 1)
                    elif k == 9:
                        act.wait_ge(d_psum[9], b + 1)
                        nc.scalar.activation(featB[:, b, :], low, ACT.Identity,
                                             bias=vecT[:, ROW_LN_BIAS:ROW_LN_BIAS + 1],
                                             scale=vecT[:, ROW_LN_SCALE:ROW_LN_SCALE + 1]).then_inc(d_out[9], 1)
                    elif k == 10:
                        act.wait_ge(d_psum[10], b + 1)
                        nc.scalar.activation(xat[:, b, :], high, ACT.Identity,
                                             bias=vecT[:, ROW_ATTN_B:ROW_ATTN_B + 1]).then_inc(d_out[10], 1)

            def tick(i):
                if i < E:
                    if i >= 2:
                        act.wait_ge(down_psum, i - 1)
                    for c in range(FC):
                        act.wait_ge(up_psum, i * FC + c // 2 * 2 + 2)
                        nc.scalar.activation(hid[:, (i % 2) * FC + c, :],
                                             bank[:, 4 + c // 2, (c % 2) * MB * P:(c % 2 + 1) * MB * P], ACT.Gelu,
                                             bias=vecT[:, ROW_B1 + i * FC + c:ROW_B1 + i * FC + c + 1]
                                             ).then_inc(hid_ready, 1)
                if 2 <= i < E + 2:
                    act.wait_ge(pre_ready, i - 1)
                    if i >= 4:
                        act.wait_ge(y_ready, i - 3)
                    nc.scalar.activation(act_out[:, i % 2, :], pre[:, i % 2, :], ACT.Gelu).then_inc(act_ready, 1)

            for what, k, slots in after_attention():
                if what == "stage":
                    stage(k, slots)
                else:
                    tick(k)

        @block.vector
        def _(dve):
            chain = [0]

            def link(ins):
                chain[0] += 1
                ins.then_inc(dve_step, 1)
                dve.wait_ge(dve_step, chain[0])

            def layer_norm_stats(k, b):
                for q in range(QT):
                    last = dve.bn_stats(stats[:, q, :], res[:, b * QT + q, :] if k < 3 else flat[:, b * QT + q, :])
                link(last)
                for q in range(QT):
                    last = dve.bn_aggr(mv[:, b * QT + q, :], stats[:, q, :])
                last.then_inc(ln_stats[k], 1)
                dve.wait_ge(ln_stats[k], b + 1)

            def layer_norm_apply(k, b):
                src, dst = (res, norm) if k < 2 else (res, flat) if k == 2 else (flat, norm)
                dve.wait_ge(ln_rstd[k], b + 1)
                for q in range(QT):
                    t = b * QT + q
                    last = dve.tensor_scalar(dst[:, t, :], src[:, t, :], mv[:, t, 0:1], rstd[:, t:t + 1],
                                             ALU.subtract, ALU.mult)
                last.then_inc(ln_done[k], 1)

            dve.memset(strip[:, 0:P - 1], 0.0)
            dve.memset(strip[:, STRIP - 1:STRIP], 0.0)
            dve.memset(v_all[:, :, :, :, HD:VW].rearrange("p b k h w -> p (b k h w)"), 1.0)
            dve.memset(bank[:, 6, 0:P], 0.0).then_inc(o_zero, 1)
            dve.wait_ge(ld_hw, 32)
            dve.tensor_scalar(hw[:, 2:3], hw[:, 0:1], -1.0, None, ALU.mult).then_inc(negw_ready, 1)
            dve.wait_ge(ld_x[0], 16)
            layer_norm_stats(0, 0)
            for b in range(B):
                if b + 1 < B:
                    dve.wait_ge(ld_x[b + 1], 16)
                    layer_norm_stats(0, b + 1)
                layer_norm_apply(0, b)
                if b == 0:
                    dve.wait_ge(e_ready, 1)
                    link(dve.tensor_scalar(hw[:, 4:5], hw[:, 3:4], 1.0, SCORE_SCALE, ALU.add, ALU.mult))
                    link(dve.tensor_scalar(dist, dist, 1.0, None, ALU.add))
                    link(dve.reciprocal(dist, dist))
                    dve.tensor_scalar(strip[:, P - 1:P - 1 + N], dist, hw[:, 4:5], None, ALU.mult
                                      ).then_inc(strip_ready, 1)
            for b in range(B):
                for qk in range(2):
                    i = 2 * b + qk
                    dve.wait_ge(qk_hi, i + 1)
                    if i >= 4:
                        dve.wait_ge(qk_lo, i - 3)
                    dve.tensor_tensor(zbuf[:, i % 4, :], bank[:, 2 + i % 4, :], parts[:, b, qk, 0, :],
                                      ALU.subtract).then_inc(qk_res, 1)
                dve.wait_ge(v_psum, b + 1)
                dve.tensor_copy(v_all[:, b, :, :, 0:HD].rearrange("p k h w -> p (k h) w"),
                                bank[:, 7, :].rearrange("p (k h w) -> p (k h) w", h=H, w=HD)
                                ).then_inc(v_ready, 1)
            dve.wait_ge(side_psum, 6)
            dve.wait_ge(ld_bc, 64)
            dve.tensor_tensor(vp[:, :, :], bank[0:CL, 5, :].rearrange("p (b d) -> p b d", d=D),
                              bv_b[0:CL, :].rearrange("p (o d) -> p o d", o=1).to_broadcast([CL, B, D]),
                              ALU.add).then_inc(side_ready, 1)
            dve.wait_ge(qk_lo, 2 * B)

            dve.wait_ge(gate_loaded, 16 * G)
            def shift(b, s):
                n = (s // HG % QT + 1) * P
                wait_batch(dve, gated, b, STEPS, s + 1)
                dve.tensor_scalar(zbuf[:, s % ZS, 0:n], zbuf[:, s % ZS, 0:n], 0.0, rowmax[:, s % ZS:s % ZS + 1],
                                  ALU.max, ALU.subtract).then_inc(shifted_even, 1)

            def batch(b):
                for s, u, g, qt, h in steps():
                    n = (qt + 1) * P
                    wait_batch(dve, turned, b, STEPS, s - ZS + 1)
                    if s % 2 == 1:
                        dve.wait_ge(rectified, b * (STEPS // 2) + s // 2 + 1)
                    else:
                        dve.wait_ge(score_ready, b * STEPS + s + 1)
                    hold(dve, dve_passed)
                    dve.tensor_tensor_reduce(zbuf[:, s % ZS, 0:n], bank[:, s % 4, 0:n],
                                             gate[:, h, 0:n][:, ::-1], 1.0, 0.0, ALU.mult, ALU.max,
                                             rowmax[:, s % ZS:s % ZS + 1]).then_inc(gated, 1)
                    if s % 2 == 1:
                        shift(b, s - 1)

            batch(0)
            with dve.Fori(1, B) as b:
                batch(b)

            def stage(k, slots):
                for b in slots:
                    ts = slice(b * QT, (b + 1) * QT)
                    low, high = bank[:, b % MB, :], bank[:, MB + b % MB, :]
                    if k == 1:
                        dve.wait_ge(ctx_saved, (b + 1) * UNITS)
                        link(dve.reciprocal(ctx_rec[:, ts, :], ctx_sum[:, ts, :, HD]))
                        dve.tensor_tensor(norm[:, ts, :].rearrange("p t (h w) -> p (t h) w", w=HD),
                                          ctx_sum[:, ts, :, 0:HD].rearrange("p t h w -> p (t h) w"),
                                          ctx_rec[:, ts, :].rearrange("p t (h o) -> p (t h) o", o=1
                                                                      ).to_broadcast([P, QT * H, HD]),
                                          ALU.mult).then_inc(d_out[0], 1)
                    elif k == 2:
                        dve.wait_ge(d_psum[2], b + 1)
                        dve.wait_ge(biased, T)
                        link(dve.tensor_tensor(res[:, ts, :], high.rearrange("p (t d) -> p t d", d=D),
                                               res[:, ts, :], ALU.add))
                        layer_norm_stats(1, b)
                    elif k == 5:
                        dve.wait_ge(d_psum[5], b + 1)
                        link(dve.tensor_reduce(xmax[:, ts], low.rearrange("p (t k) -> p t k", k=P)[:, :, 0:CL],
                                               AX.X, ALU.max))
                        dve.tensor_scalar(xmax[:, ts], xmax[:, ts], -X_SCALE, None, ALU.mult
                                          ).then_inc(xmax_ready, 1)
                    elif k == 6:
                        dve.wait_ge(d_psum[6], b + 1)
                        dve.tensor_copy(xprobT[:, b, :], high[0:CL, :]).then_inc(d_out[6], 1)
                    elif k == 8:
                        dve.wait_ge(d_out[5], b + 1)
                        link(dve.reciprocal(xrec[:, ts], xsum[:, ts]))
                        dve.wait_ge(biased, T + (b + 1) * QT)
                        dve.wait_ge(d_psum[8], b + 1)
                        for q in range(QT):
                            t = b * QT + q
                            last = dve.scalar_tensor_tensor(out=res[:, t, :], in0=high[:, q * P:(q + 1) * P],
                                                            scalar=xrec[:, t:t + 1], in1=res[:, t, :],
                                                            op0=ALU.mult, op1=ALU.add)
                        link(last)
                        layer_norm_stats(2, b)
                if k == 2:
                    for b in slots:
                        layer_norm_apply(1, b)
                elif k == 8:
                    for b in slots:
                        layer_norm_apply(2, b)
                        dve.wait_ge(ln_done[2], b + 1)
                        layer_norm_stats(3, b)
                    for b in slots:
                        layer_norm_apply(3, b)

            def tick(i):
                if 2 <= i < E + 2:
                    f = i - 2
                    dve.wait_ge(next_psum, f + 1)
                    if f >= 2:
                        dve.wait_ge(act_ready, f - 1)
                    dve.tensor_tensor(pre[:, f % 2, :].rearrange("p (m d) -> p m d", d=D),
                                      bank[:, 7, 0:MB * D].rearrange("p (m d) -> p m d", d=D),
                                      nb_b[:, :].rearrange("p (o d) -> p o d", o=1).to_broadcast([P, MB, D]),
                                      ALU.add).then_inc(pre_ready, 1)
                if i >= 3:
                    f = i - 3
                    dve.wait_ge(act_ready, f + 1)
                    if f >= 2:
                        dve.wait_ge(y_stored[f % 2], 16 * (f // 2))
                    dve.tensor_tensor(y_out[:, f % 2, :].rearrange("p (m d) -> p m d", d=D),
                                      act_out[:, f % 2, :].rearrange("p (m d) -> p m d", d=D),
                                      res_v[:, f // QT * MB:(f // QT + 1) * MB, f % QT, :], ALU.add
                                      ).then_inc(y_ready, 1)
                if 1 <= i < E + 1:
                    f = i - 1
                    dve.wait_ge(down_psum, f + 1)
                    if f >= 2:
                        dve.wait_ge(next_psum, f - 1)
                    dve.tensor_scalar(eo[:, f % 2, :], bank[:, 6, 0:MB * P],
                                      vecT[:, ROW_B2 + f:ROW_B2 + f + 1], None, ALU.add).then_inc(eo_ready, 1)

            for what, k, slots in after_attention():
                if what == "stage":
                    stage(k, slots)
                else:
                    tick(k)

        @block.tensor
        def _(pe):
            mm, turn = nc.tensor.matmul, nc.tensor.transpose
            pe.wait_ge(ident_ready, 1)
            pe.wait_ge(ld_proj, 48)
            for b in range(B):
                pe.wait_ge(ln_done[0], b + 1)
                if b >= 2:
                    pe.wait_ge(xnT_ready, b - 1)
                for q in range(QT):
                    last = turn(bank[:, b % 2, q * P:(q + 1) * P], norm[:, b * QT + q, :], ident[:, :])
                last.then_inc(xnT_psum, 1)
                pe.wait_ge(xnT_ready, b + 1)
                for i, w in ((2 * b, wq), (2 * b + 1, wk)):
                    if i >= 4:
                        pe.wait_ge(qk_res, i - 3)
                    mm(bank[:, 2 + i % 4, :], w[:, :], featA[:, b, :], start=True, stop=True).then_inc(qk_psum, 1)
                if b >= 1:
                    pe.wait_ge(v_ready, b)
                for q in range(QT):
                    last = mm(bank[:, 7, q * P:(q + 1) * P], featA[:, b, q * P:(q + 1) * P], wv[:, :],
                              start=True, stop=True)
                last.then_inc(v_psum, 1)
            pe.wait_ge(ld_vec, 96)
            pe.wait_ge(xnT_ready, B)
            turn(bank[:, 0, 0:VEC_ROWS], vecs[:, :], ident[0:VEC_ROWS, 0:VEC_ROWS]).then_inc(side_psum, 1)
            pe.wait_ge(ld_raw, 96)
            for i in range(4):
                last = turn(bank[:, 1, i * P:(i + 1) * P], raw_w[:, i, :], ident[:, :])
            last.then_inc(side_psum, 1)
            pe.wait_ge(qk_res, 2 * B)
            for i in range(2):
                last = turn(bank[:, 2, i * P:(i + 1) * P], raw_w[:, 4 + i, :], ident[:, :])
            last.then_inc(side_psum, 1)
            pe.wait_ge(ld_ctx, 16 * B)
            for b in range(B):
                last = turn(bank[:, 3, b * CL:(b + 1) * CL], ctx_in[:, b, :], ident[0:CL, 0:CL])
            last.then_inc(side_psum, 1)
            pe.wait_ge(side_ready, 4)
            mm(bank[:, 4, 0:B * CL], wT[:, XWK, :], ctxT[:, :, :].rearrange("p b s -> p (b s)"),
               start=True, stop=True).then_inc(side_psum, 1)
            for b in range(B):
                last = mm(bank[0:CL, 5, b * P:(b + 1) * P], ctxT[:, b, :], wT[:, XWV, :], start=True, stop=True)
            last.then_inc(side_psum, 1)
            pe.wait_ge(side_ready, 6)
            pe.wait_ge(v_ready, B)
            pe.wait_ge(o_zero, 1)

            plan = list(steps())
            LAG = 2

            def scores(b, s):
                _, u, g, qt, h = plan[s]
                n, i, j = (qt + 1) * P, h % 2, h // 2
                if s % (QT * HG) == 0:
                    pe.wait_ge(stack_loaded[g], b * 64 + 64)
                wait_batch(pe, gated, b, STEPS, s - 3)
                r = slice(64 * i, 64 * i + SLOTS * HD)
                mm(bank[:, s % 4, 0:n], q_stack[r, j, qt * P:(qt + 1) * P], k_stack[r, j, 0:n],
                   start=True, stop=True).then_inc(score_ready, 1)

            def turn_step(b, s):
                if isinstance(b, int) and b * STEPS + s < 0:
                    return
                qt = s // HG % QT
                wait_batch(pe, shifted_odd if s % 2 else shifted_even, b, STEPS // 2, s // 2 + 1)
                wait_batch(pe, exped, b, STEPS, s - 1)
                for k in range(qt + 1):
                    last = turn(bank[:, 4 + s % 2, k * P:(k + 1) * P], zbuf[:, s % ZS, k * P:(k + 1) * P],
                                ident[:, :])
                last.then_inc(turned, 1)

            def values(b, u):
                if isinstance(b, int) and b * UNITS + u < 0:
                    return
                g, qt = u % UNITS // QT, u % QT
                wait_batch(pe, masked, b, UNITS, u + 1)
                wait_batch(pe, o_copied, b, UNITS, u)
                if qt == 0:
                    wait_batch(pe, v_copied, b, G, g + 1)
                for k in range(qt + 1):
                    for i in range(HG):
                        last = mm(bank[32 * i:32 * i + VW, 6, 0:P], v_cur[:, k, g * HG + i, :],
                                  probT[:, (u % 2) * HG + i, k * P:(k + 1) * P],
                                  start=(k == 0), stop=(k == qt))
                last.then_inc(pv_done, 1)

            def turn_context(b, u):
                if isinstance(b, int) and b * UNITS + u < 0:
                    return
                wait_batch(pe, o_copied, b, UNITS, u + 1)
                wait_batch(pe, ctx_saved, b, UNITS, u)
                turn(bank[:, 7, 0:P], o_sb[:, u % 2, :], ident[:, :]).then_inc(o_turned, 1)

            def batch(b, last_batch):
                for s in range(STEPS):
                    if s + 3 < STEPS:
                        scores(b, s + 3)
                    elif not last_batch:
                        scores(b + 1, s + 3 - STEPS)
                    turn_step(b, s - LAG)
                    if s % HG == 0:
                        values(b, s // HG - 2)
                    if s % HG == 2:
                        turn_context(b, s // HG - 2)

            for s in range(3):
                scores(0, s)
            batch(0, False)
            with pe.Fori(1, B - 1) as b:
                batch(b, False)
            batch(B - 1, True)
            for s in range(-LAG, 0):
                turn_step(B, s)
            values(B, -2)
            turn_context(B, -2)
            values(B, -1)
            turn_context(B, -1)

            def stage(k, slots):
                for b in slots:
                    low, high = bank[:, b % MB, :], bank[:, MB + b % MB, :]
                    tiles = [(slice(q * P, (q + 1) * P), b * QT + q) for q in range(QT)]
                    if k in (1, 3, 9):
                        pe.wait_ge(*{1: (d_out[0], b + 1), 3: (ln_done[1], b + 1), 9: (ln_done[3], b + 1)}[k])
                        for cols, t in tiles:
                            last = turn(low[:, cols], norm[:, t, :], ident[:, :])
                    elif k == 2:
                        pe.wait_ge(d_out[1], b + 1)
                        if b >= MB:
                            pe.wait_ge(d_out[10], b - MB + 1)
                        for cols, t in tiles:
                            last = mm(high[:, cols], featA[:, b, cols], wo[:, :], start=True, stop=True)
                    elif k == 4:
                        pe.wait_ge(d_out[3], b + 1)
                        last = mm(high, wT[:, XWQ, :], featA[:, b, :], start=True, stop=True)
                    elif k == 5:
                        pe.wait_ge(d_out[4], b + 1)
                        for cols, t in tiles:
                            last = mm(low[:, cols.start:cols.start + CL], featB[:, b, cols], kpT[:, b, :],
                                      start=True, stop=True)
                    elif k == 6:
                        pe.wait_ge(d_out[5], b + 1)
                        for cols, t in tiles:
                            last = turn(high[0:CL, cols], xprob[:, b, cols.start:cols.start + CL], ident[:, :])
                    elif k == 7:
                        pe.wait_ge(d_out[6], b + 1)
                        last = mm(low, vp[:, b, :], xprobT[:, b, :], start=True, stop=True)
                    elif k == 8:
                        pe.wait_ge(d_out[7], b + 1)
                        for cols, t in tiles:
                            last = mm(high[:, cols], featA[:, b, cols], wT[:, XWO, :], start=True, stop=True)
                    elif k == 10:
                        pe.wait_ge(d_out[9], b + 1)
                        mm(high, wT[:, FAW, :], featB[:, b, :], start=True, stop=False, skip_group_check=True)
                        for cols, t in tiles:
                            last = mm(high[:, cols], flat[:, t, :], ident[:, :], start=False,
                                      stop=(t % QT == QT - 1), skip_group_check=True)
                    last.then_inc(d_psum[k], 1)

            def tick(i):
                if i < E:
                    p, q = i // QT, i % QT
                    if i == 0:
                        pe.wait_ge(ld_ffn, 32)
                    pe.wait_ge(d_out[10], (p + 1) * MB)
                    for c in range(FC):
                        if i >= 1 and c % 2 == 0:
                            pe.wait_ge(hid_ready, (i - 1) * FC + c + 2)
                        mm(bank[:, 4 + c // 2, (c % 2) * MB * P:(c % 2 + 1) * MB * P], w1[:, i, c * P:(c + 1) * P],
                           xat[:, p * MB:(p + 1) * MB, q * P:(q + 1) * P], start=True, stop=True
                           ).then_inc(up_psum, 1)
                if 2 <= i < E + 2:
                    f = i - 2
                    pe.wait_ge(eo_ready, f + 1)
                    if f >= 1:
                        pe.wait_ge(pre_ready, f)
                    for m in range(MB):
                        last = mm(bank[:, 7, m * P:(m + 1) * P], eo[:, f % 2, m * P:(m + 1) * P],
                                  wT[:, FNW, :], start=True, stop=True)
                    last.then_inc(next_psum, 1)
                if 1 <= i < E + 1:
                    f = i - 1
                    if f >= 1:
                        pe.wait_ge(eo_ready, f)
                    for c in range(FC):
                        pe.wait_ge(hid_ready, f * FC + c + 1)
                        last = mm(bank[:, 6, 0:MB * P], w2[:, f, c, :], hid[:, (f % 2) * FC + c, :],
                                  start=(c == 0), stop=(c == FC - 1))
                    last.then_inc(down_psum, 1)

            for what, k, slots in after_attention():
                if what == "stage":
                    stage(k, slots)
                else:
                    tick(k)


_INS = ['x', 'ctx_1024', 'L0_attn_Wq', 'L0_attn_Wk', 'L0_attn_Wv', 'L0_attn_Wo', 'L0_attn_bo', 'L0_attn_w',
        'L0_attn_v', 'L0_xattn_Wk', 'L0_xattn_Wv', 'L0_xattn_bv', 'L0_xattn_Wq', 'L0_xattn_bq', 'L0_xattn_Wo',
        'L0_xattn_bo', 'L0_ffn_ln_scale', 'L0_ffn_ln_bias', 'L0_ffn_attn_w', 'L0_ffn_attn_b', 'L0_ffn_w1',
        'L0_ffn_b1', 'L0_ffn_w2', 'L0_ffn_b2', 'L0_ffn_next_w', 'L0_ffn_next_b']


def kernel(**inputs):
    import numpy as _np
    import concourse.bacc as _bacc
    from concourse import mybir as _mybir
    from concourse.bass_utils import run_bass_kernel_spmd as _run

    nc = _bacc.Bacc("TRN2", target_bir_lowering=False, num_devices=1)
    arrays, args = {}, []
    for name in _INS:
        a = _np.ascontiguousarray(inputs[name])
        arrays[f"in_{name}"] = a
        args.append(nc.dram_tensor(f"in_{name}", a.shape, _mybir.dt.from_np(a.dtype), kind="ExternalInput").ap())
    shape = tuple(inputs["x"].shape)
    args.append(nc.dram_tensor("out_x", shape, _mybir.dt.float32, kind="ExternalOutput").ap())
    decoder_kernel(nc, *args)
    r = _run(nc, [arrays], core_ids=[0])
    return r.results[0]["out_x"]
```

```python
from contextlib import ExitStack

import concourse.bass as bass
from concourse import mybir

ALU = mybir.AluOpType
ACT = mybir.ActivationFunctionType
AX = mybir.AxisListType
F32 = mybir.dt.float32
BF16 = mybir.dt.bfloat16

P = 128
LN_EPS = 1e-5
Q_PART = (0, 0, 0, 1, 1, 2)
K_PART = (0, 1, 2, 0, 1, 0)
SLOTS = len(Q_PART)
ROW_B1, ROW_B2, ROW_XBQ, ROW_LN_SCALE, ROW_LN_BIAS, ROW_ATTN_B, VEC_ROWS = 0, 32, 40, 41, 42, 43, 44


def decoder_kernel(nc, x, ctx_1024, L0_attn_Wq, L0_attn_Wk, L0_attn_Wv, L0_attn_Wo, L0_attn_bo, L0_attn_w,
                   L0_attn_v, L0_xattn_Wk, L0_xattn_Wv, L0_xattn_bv, L0_xattn_Wq, L0_xattn_bq, L0_xattn_Wo,
                   L0_xattn_bo, L0_ffn_ln_scale, L0_ffn_ln_bias, L0_ffn_attn_w, L0_ffn_attn_b, L0_ffn_w1,
                   L0_ffn_b1, L0_ffn_w2, L0_ffn_b2, L0_ffn_next_w, L0_ffn_next_b, out):
    B, N, D = x.shape
    H = L0_attn_w.shape[0]
    HD = D // H
    CL = ctx_1024.shape[1]
    E, _, FF = L0_ffn_w1.shape
    QT = N // P
    T = B * QT
    FC = FF // P
    HG = 4
    G = H // HG
    UNITS = G * QT
    STEPS = UNITS * HG
    VW = HD + 1
    MB = T // E
    STRIP = N + P
    PAIRS = E // QT
    BATCH_OF = [m * PAIRS + p for p in range(PAIRS) for m in range(MB)]
    ZS = 8
    SCORE_SCALE = 1.0 / float(HD) ** 0.5
    X_SCALE = 1.0 / float(D) ** 0.5
    FRONT = ("stats", "norm", "turn", "q", "k", "v", "parts")
    SIDE = ("vectors", "weights", "weights2", "context", "xkeys", "xvalues")
    STAGES = ("context", "context_turn", "attn_out", "xnorm", "xnorm_turn", "xquery", "xscore", "xprob_turn", "xcontext",
              "xout", "flat", "fnorm", "fnorm_turn", "xattn")
    XBIAS = STAGES[4:4 + QT]
    BIAS_AT = 10
    VALUE_BLOCKS = [(range((qt + 1) // 2), range((qt + 1) // 2, qt + 1)) for qt in range(QT)]
    TURN_LAG = 2
    SCORES_AHEAD = 3
    RECTIFY_AHEAD = 5
    WARM_UP = 18
    HOSTED = 2
    EXPERT_STAGES = ("xnorm", "xout", "flat", "fnorm")
    SPARE = 7
    assert D == P and T % E == 0 and HG * 32 == P and PAIRS * MB == B and MB == 2

    with ExitStack() as ctx:
        def sb(name, shape, dt=F32):
            return ctx.enter_context(nc.sbuf_tensor(name, shape, dt))

        def sem(name):
            return ctx.enter_context(nc.semaphore(name))

        strip_dram = nc.dram_tensor("strip_scratch", [H, STRIP], F32, kind="Internal").ap()
        stack_dram = nc.dram_tensor("stack_scratch", [B, 2, H, HD, SLOTS, N], BF16, kind="Internal").ap()

        bank = ctx.enter_context(nc.psum_tensor("bank", [P, 8, 512], F32))

        ident = sb("ident", [P, P])
        res = sb("res", [P, T, D])
        norm = sb("norm", [P, T, D])
        flat = sb("flat", [P, T, D])
        featA = sb("featA", [P, B, N])
        featB = sb("featB", [P, B, N])
        xat = sb("xat", [P, B, N])
        stats = sb("stats", [P, QT, 6])
        mv = sb("mv", [P, T, 2])
        rstd = sb("rstd", [P, T])
        rstd2 = sb("rstd2", [P, T])
        mhalf = sb("mhalf", [P, QT])
        parts = sb("parts", [P, B, 2, 3, N], BF16)
        qk_stack = sb("qk_stack", [P, 2, H // 2, N], BF16)
        gate = sb("gate", [P, H, N])
        zbuf = sb("zbuf", [P, ZS, N])
        probT = sb("probT", [P, 2 * HG, N])
        v_all = sb("v_all", [P, B, QT, H, VW])
        v_cur = sb("v_cur", [P, QT, H, VW])
        rowmax = sb("rowmax", [P, ZS])
        o_sb = sb("o_sb", [P, 2, P])
        ctx_sum = sb("ctx_sum", [P, T, H, VW])
        ctx_rec = sb("ctx_rec", [P, T, H])
        wq = sb("wq", [P, D])
        wk = sb("wk", [P, D])
        wv = sb("wv", [P, D])
        wo = sb("wo", [P, D])
        wT = sb("wT", [P, 6, D])
        XWK, XWV, XWQ, XWO, FAW, FNW = range(6)
        vecs = sb("vecs", [VEC_ROWS, P])
        vecT = sb("vecT", [P, VEC_ROWS])
        bo_b = sb("bo_b", [P, D])
        bv_b = sb("bv_b", [P, D])
        xbo_b = sb("xbo_b", [P, D])
        nb_b = sb("nb_b", [P, D])
        ctx_in = sb("ctx_in", [CL, B, D])
        ctxT = sb("ctxT", [P, B, CL])
        kpT = sb("kpT", [P, B, CL])
        vp = sb("vp", [CL, B, D])
        xmax = sb("xmax", [P, T])
        xsum = sb("xsum", [P, T])
        xrec = sb("xrec", [P, T])
        w1 = sb("w1", [P, E, FF])
        hw = sb("hw", [H, 8])
        raw_w = flat[:, 0:6, :]
        residue = flat[:, 8:16, :].rearrange("p (i t) d -> p i (t d)", i=2)
        dist = xat[0:H, 0, :]
        strip = xat[0:H, 1:3, :].rearrange("h a n -> h (a n)")[:, 0:STRIP]
        xprob = featB
        xprobT = featA[0:CL, :, :]
        w2 = parts[:, :, :, :, :].rearrange("p b k r n -> p (b k r n)").bitcast(F32)[:, 0:E * FC * D].rearrange(
            "p (e c d) -> p e c d", e=E, c=FC)
        hid = gate[:, 0:4, :].rearrange("p a (c n) -> p (a c) n", c=2)
        eo = gate[:, 4:5, :].rearrange("p a (c n) -> p (a c) n", c=2)
        pre = gate[:, 5:6, :].rearrange("p a (c n) -> p (a c) n", c=2)
        act_out = gate[:, 6:7, :].rearrange("p a (c n) -> p (a c) n", c=2)
        y_out = gate[:, 7:8, :].rearrange("p a (c n) -> p (a c) n", c=2)

        ld_x = [sem(f"ld_x{b}") for b in range(B)]
        ld_hw, ld_proj, ld_vec, ld_raw, ld_bc, ld_ctx, ld_wo, ld_ffn = (
            sem(n) for n in ("ld_hw", "ld_proj", "ld_vec", "ld_raw", "ld_bc", "ld_ctx", "ld_wo", "ld_ffn"))
        pool_step, dve_step = sem("pool_step"), sem("dve_step")
        ident_ready, dist_ready, e_ready, strip_ready = (
            sem(n) for n in ("ident_ready", "dist_ready", "e_ready", "strip_ready"))
        negw_ready = sem("negw_ready")
        strip_written = sem("strip_written")
        gate_loaded = [sem(f"gate_loaded{g}") for g in range(G)]
        ln_stats, ln_rstd, ln_done = ([sem(f"{n}{k}") for k in range(4)] for n in ("ln_stats", "ln_rstd", "ln_done"))
        xnT_psum, xnT_ready = sem("xnT_psum"), sem("xnT_ready")
        qk_psum, qk_hi, qk_res, qk_mid, qk_lo = (
            sem(n) for n in ("qk_psum", "qk_hi", "qk_res", "qk_mid", "qk_lo"))
        v_psum, v_ready = sem("v_psum"), sem("v_ready")
        side_psum, side_ready = sem("side_psum"), sem("side_ready")
        biased = sem("biased")
        xbiased = [sem(f"xbiased{b}") for b in range(B)]
        first_written, stack_written = sem("first_written"), sem("stack_written")
        stack_loaded = [sem(f"stack_loaded{g}") for g in range(G)]
        v_copied, o_zero = sem("v_copied"), sem("o_zero")
        score_ready, rectified, gated, shifted_even, shifted_odd, turned = (
            sem(n) for n in ("score_ready", "rectified", "gated", "shifted_even", "shifted_odd", "turned"))
        exped, masked, pv_done, o_copied, o_turned, ctx_saved = (
            sem(n) for n in ("exped", "masked", "pv_done", "o_copied", "o_turned", "ctx_saved"))
        d_psum = {name: sem(f"psum_{name}") for name in STAGES}
        d_out = {name: sem(f"out_{name}") for name in STAGES}
        dve_passed, pool_passed = sem("dve_passed"), sem("pool_passed")
        xmax_ready = sem("xmax_ready")
        up_psum, hid_ready, down_psum, eo_ready, next_psum, pre_ready, act_ready, y_ready = (
            sem(n) for n in ("up_psum", "hid_ready", "down_psum", "eo_ready", "next_psum", "pre_ready",
                             "act_ready", "y_ready"))
        y_stored = [sem("y_stored0"), sem("y_stored1")]

        x_v = x.rearrange("b (q p) d -> b p q d", p=P)
        out_v = out.rearrange("b (q p) d -> q p b d", p=P)
        res_v = res[:, :, :].rearrange("p (b q) d -> p b q d", q=QT)

        def steps():
            for s in range(STEPS):
                u = s // HG
                yield s, u, u // QT, u % QT, (u // QT) * HG + s % HG

        def wait_batch(eng, signal, b, per_batch, k):
            if isinstance(b, int) and b * per_batch + k <= 0:
                return
            eng.wait_ge(signal, b * per_batch + k)

        def hold(eng, passed):
            eng.sem_inc(passed, 1)

        PE_DELAY = {0: 0, B - 1: 0}
        ACT_DELAY = {0: -TURN_LAG, B - 1: -TURN_LAG}
        DVE_DELAY = {0: 3, B - 1: 2}
        POOL_DELAY = {0: 1, B - 1: 2}

        def front_bank(name, b):
            return {("turn", 0): 3, ("q", 0): 4, ("k", 0): 5, ("turn", 1): 0, ("q", 1): 1, ("k", 1): 2
                    }.get((name, b), SPARE)

        def stage_banks(b):
            return (bank[:, SPARE, :], bank[:, SPARE, :]) if b < HOSTED else (bank[:, b % 2, :], bank[:, 2 + b % 2, :])

        def spread(items, first, every):
            return [(first + int(i * every), item) for i, item in enumerate(items)]

        BEFORE = [("stats", 0), ("norm", 0), ("stats", 1), ("turn", 0), ("q", 0), ("k", 0), ("parts", 0), ("v", 0),
                  ("norm", 1), ("turn", 1), ("stats", 2), ("q", 1), ("k", 1), ("v", 1), ("parts", 1), ("norm", 2)]
        BESIDE = {
            0: spread([(name, b) for b in range(2, B) for name in FRONT if (name, b) not in BEFORE]
                      + [(name, None) for name in SIDE], 0, 3.5),
            B - 1: spread([(name, b) for name in STAGES for b in range(HOSTED)], 5, 2),
        }

        def beside(b, s, delay):
            if isinstance(b, int):
                for at, item in BESIDE.get(b, []):
                    if min(max(at + delay[b], 0), STEPS - 1) == s:
                        yield item

        def after_attention():
            tick = 0
            for name in STAGES:
                yield "stage", name
                if name in EXPERT_STAGES:
                    yield "tick", tick
                    tick += 1
            while tick < E + 3:
                yield "tick", tick
                tick += 1

        block = ctx.enter_context(nc.Block())

        @block.sync
        def _(sp):
            sp.dma_start(res[:, 0:QT, :], x_v[BATCH_OF[0]]).then_inc(ld_x[0], 16)
            sp.dma_start(hw[:, 0:1], L0_attn_w.rearrange("(h o) -> h o", o=1)).then_inc(ld_hw, 16)
            sp.dma_start(hw[:, 1:2], L0_attn_v.rearrange("(h o) -> h o", o=1)).then_inc(ld_hw, 16)
            for dst, src in ((wq, L0_attn_Wq), (wk, L0_attn_Wk), (wv, L0_attn_Wv)):
                sp.dma_start(dst[:, :], src).then_inc(ld_proj, 16)
            for b in range(1, B):
                sp.dma_start(res[:, b * QT:(b + 1) * QT, :], x_v[BATCH_OF[b]]).then_inc(ld_x[b], 16)
            for dst, src in ((bo_b, L0_attn_bo), (bv_b, L0_xattn_bv), (xbo_b, L0_xattn_bo),
                             (nb_b, L0_ffn_next_b)):
                sp.dma_start(dst[:, :], bass.AP(tensor=src.tensor, offset=0, ap=[[0, P], [1, D]])
                             ).then_inc(ld_bc, 16)
            for i, src in enumerate((L0_xattn_Wk, L0_xattn_Wv, L0_xattn_Wq, L0_xattn_Wo, L0_ffn_attn_w,
                                     L0_ffn_next_w)):
                sp.dma_start(raw_w[:, i, :], src).then_inc(ld_raw, 16)

            def write_stack(b, heads, written):
                rows = slice(heads.start * HD, heads.stop * HD)
                sp.wait_ge(qk_lo, b * 2 + 1)
                for slot, run in ((0, 3), (3, 2), (5, 1)):
                    q_part = Q_PART[slot]
                    sp.dma_start(stack_dram[b, 0, heads, :, slot:slot + run, :].rearrange("h d s t -> (h d) s t"),
                                 parts[rows, b, 0, q_part:q_part + 1, :].to_broadcast([rows.stop - rows.start, run, N])
                                 ).then_inc(written, 16)
                sp.wait_ge(qk_lo, b * 2 + 2)
                for slot, run in ((0, 3), (3, 2), (5, 1)):
                    k_part = K_PART[slot]
                    sp.dma_start(stack_dram[b, 1, heads, :, slot:slot + run, :].rearrange("h d s t -> (h d) s t"),
                                 parts[rows, b, 1, k_part:k_part + run, :]).then_inc(written, 16)

            def read_stack(b, g):
                for i in range(2):
                    h0 = g * HG + i
                    for qk in range(2):
                        sp.dma_start(qk_stack[64 * i:64 * i + SLOTS * HD, qk, 2 * g:2 * g + 2, :],
                                     stack_dram[b, qk, h0:h0 + 3:2, :, :, :].rearrange("h d s t -> (d s) h t")
                                     ).then_inc(stack_loaded[g], 16)

            sp.wait_ge(strip_ready, 1)
            sp.dma_start(strip_dram, strip).then_inc(strip_written, 16)
            sp.wait_ge(strip_written, 16)

            def read_gate(g):
                sp.dma_start(gate[:, g * HG:(g + 1) * HG, :],
                             bass.AP(tensor=strip_dram.tensor, offset=g * HG * STRIP,
                                     ap=[[1, P], [STRIP, HG], [1, N]])).then_inc(gate_loaded[g], 16)

            read_gate(0)
            write_stack(0, slice(0, HG), first_written)
            sp.wait_ge(first_written, 96)
            read_stack(0, 0)
            write_stack(0, slice(HG, H), stack_written)
            read_gate(1)
            sp.wait_ge(stack_written, 96)
            read_stack(0, 1)
            for g in range(2, G):
                read_gate(g)
                read_stack(0, g)
            sp.dma_start(vecs[ROW_B1:ROW_B1 + E * FC, :],
                         L0_ffn_b1.rearrange("e (c p) -> (e c) p", p=P)).then_inc(ld_vec, 16)
            sp.dma_start(vecs[ROW_B2:ROW_B2 + E, :], L0_ffn_b2).then_inc(ld_vec, 16)
            for row, src in ((ROW_XBQ, L0_xattn_bq), (ROW_LN_SCALE, L0_ffn_ln_scale),
                             (ROW_LN_BIAS, L0_ffn_ln_bias), (ROW_ATTN_B, L0_ffn_attn_b)):
                sp.dma_start(vecs[row:row + 1, :], src.rearrange("(o d) -> o d", o=1)).then_inc(ld_vec, 16)
            for b in range(B):
                sp.dma_start(ctx_in[:, b, :], ctx_1024[BATCH_OF[b]]).then_inc(ld_ctx, 16)
            sp.dma_start(wo[:, :], L0_attn_Wo).then_inc(ld_wo, 16)
            with sp.Fori(1, B) as b:
                write_stack(b, slice(0, H), stack_written)
                sp.wait_ge(stack_written, b * 96 + 96)
                for g in range(G):
                    sp.wait_ge(score_ready, b * STEPS - STEPS + (g + 1) * QT * HG)
                    read_stack(b, g)
            sp.dma_start(w1[:, :, :], L0_ffn_w1.rearrange("e d f -> d e f")).then_inc(ld_ffn, 16)
            sp.dma_start(w2[:, :, :, :], L0_ffn_w2.rearrange("e (c p) d -> p e c d", p=P)).then_inc(ld_ffn, 16)
            for e in range(E):
                sp.wait_ge(y_ready, e + 1)
                sp.dma_start(out_v[e % QT, :, e // QT:B:PAIRS, :], y_out[:, e % 2, :].rearrange("p (m d) -> p m d", d=D)
                             ).then_inc(y_stored[e % 2], 16)
            for i in range(2):
                sp.wait_ge(y_stored[i], 16 * (E // 2))

        @block.gpsimd
        def _(pool):
            pool.memset(ident[:, :], 0.0).then_inc(pool_step, 1)
            pool.memset(mhalf[:, :], -0.5)
            pool.iota(dist, pattern=[[1, N]], base=0, channel_multiplier=0,
                      allow_small_or_imprecise_dtypes=True).then_inc(dist_ready, 1)
            pool.wait_ge(pool_step, 1)
            pool.affine_select(out=ident[:, :], in_=ident[:, :], compare_op=ALU.not_equal, fill=1.0, base=0,
                               pattern=[[-1, P]], channel_multiplier=1).then_inc(ident_ready, 1)
            steps_done = [1]

            def link(ins):
                steps_done[0] += 1
                ins.then_inc(pool_step, 1)
                pool.wait_ge(pool_step, steps_done[0])

            def layer_norm_rstd(k, b):
                ts = slice(b * QT, (b + 1) * QT)
                pool.wait_ge(ln_stats[k], b + 1)
                link(pool.tensor_scalar(rstd[:, ts], mv[:, ts, 1], LN_EPS, 1.0, ALU.add, ALU.mult))
                pool.tensor_tensor(rstd[:, ts], rstd[:, ts], mhalf[:, :], ALU.pow).then_inc(ln_rstd[k], 1)

            def second_norm_rstd(b):
                ts = slice(b * QT, (b + 1) * QT)
                pool.wait_ge(ln_rstd[2], b + 1)
                link(pool.tensor_tensor(rstd2[:, ts], rstd[:, ts], rstd[:, ts], ALU.mult))
                link(pool.tensor_tensor(rstd2[:, ts], rstd2[:, ts], mv[:, ts, 1], ALU.mult))
                link(pool.tensor_scalar(rstd2[:, ts], rstd2[:, ts], LN_EPS, 1.0, ALU.add, ALU.mult))
                pool.tensor_tensor(rstd2[:, ts], rstd2[:, ts], mhalf[:, :], ALU.pow).then_inc(ln_rstd[3], 1)

            def low_part(i):
                b, qk = i // 2, i % 2
                pool.wait_ge(qk_mid, i + 1)
                pool.tensor_tensor(parts[:, b, qk, 2, :], residue[:, i % 2, :], parts[:, b, qk, 1, :],
                                   ALU.subtract).then_inc(qk_lo, 1)

            def front(name, b):
                if name == "stats":
                    layer_norm_rstd(0, b)
                elif name == "v" and b:
                    low_part(2 * b)
                elif name == "parts" and b:
                    low_part(2 * b + 1)

            def stage(name, b):
                if name == "attn_out":
                    layer_norm_rstd(1, b)
                elif name in XBIAS:
                    t = b * QT + XBIAS.index(name)
                    pool.wait_ge(ln_done[1], t + 1)
                    pool.tensor_tensor(res[:, t, :], res[:, t, :], xbo_b[:, :], ALU.add).then_inc(xbiased[b], 1)
                elif name == "xout":
                    layer_norm_rstd(2, b)
                    second_norm_rstd(b)

            for name, slot in BEFORE:
                front(name, slot)

            def mask(b, u):
                if isinstance(b, int) and b * UNITS + u < 0:
                    return
                qt = u % QT
                wait_batch(pool, exped, b, STEPS, HG * (u + 1))
                hold(pool, pool_passed)
                diag = probT[:, (u % 2) * HG:(u % 2) * HG + HG, qt * P:(qt + 1) * P]
                pool.affine_select(out=diag, in_=diag, compare_op=ALU.is_ge, fill=0.0, base=0,
                                   pattern=[[0, HG], [1, P]], channel_multiplier=-1).then_inc(masked, 1)

            def batch(b):
                for s, u, g, qt, h in steps():
                    n = (qt + 1) * P
                    if s % (QT * HG) == 0:
                        pool.wait_ge(v_ready, b + 1)
                        wait_batch(pool, pv_done, b, UNITS, (g + 1) * QT - UNITS)
                        hs = slice(g * HG, (g + 1) * HG)
                        pool.tensor_copy(v_cur[:, :, hs, :].rearrange("p k h w -> p k (h w)"),
                                         v_all[:, b, :, hs, :].rearrange("p k h w -> p k (h w)")
                                         ).then_inc(v_copied, 1)
                    if s % 2 == 1:
                        pool.wait_ge(gated, b * STEPS + s + 1)
                        hold(pool, pool_passed)
                        pool.tensor_scalar(zbuf[:, s % ZS, 0:n], zbuf[:, s % ZS, 0:n], -1.0,
                                           rowmax[:, s % ZS:s % ZS + 1], ALU.mult, ALU.add
                                           ).then_inc(shifted_odd, 1)
                    if s % HG == 1:
                        mask(b, u - 1)
                    if s % (STEPS // QT) == BIAS_AT:
                        if isinstance(b, int) and b == 0 and s == BIAS_AT:
                            pool.wait_ge(ld_bc, 64)
                        t = b * QT + s // (STEPS // QT)
                        pool.wait_ge(ln_done[0], (b + 1) * QT)
                        hold(pool, pool_passed)
                        pool.tensor_tensor(res[:, t, :], res[:, t, :], bo_b[:, :], ALU.add).then_inc(biased, 1)
                    for name, slot in beside(b, s, POOL_DELAY):
                        (front if b == 0 else stage)(name, slot)

            batch(0)
            with pool.Fori(1, B - 1) as b:
                batch(b)
            batch(B - 1)
            mask(B, -1)

            for what, which in after_attention():
                if what == "stage":
                    for b in range(HOSTED, B):
                        stage(which, b)

        @block.scalar
        def _(act):
            def o_copy(b, u):
                if isinstance(b, int) and b * UNITS + u < 0:
                    return
                wait_batch(act, pv_done, b, UNITS, u + 1)
                wait_batch(act, o_turned, b, UNITS, u - 1)
                nc.scalar.copy(o_sb[:, u % 2, :], bank[:, 6, 0:P]).then_inc(o_copied, 1)

            def ctx_save(b, u):
                if isinstance(b, int) and b * UNITS + u < 0:
                    return
                tile = b * QT + u % QT if u >= 0 else b * QT - QT + u % QT
                g = u % UNITS // QT
                wait_batch(act, o_turned, b, UNITS, u + 1)
                nc.scalar.copy(ctx_sum[:, tile, g * HG:(g + 1) * HG, :],
                               bank[:, 6, P:2 * P].rearrange("p (h w) -> p h w", w=32)[:, :, 0:VW]
                               ).then_inc(ctx_saved, 1)

            act.wait_ge(ld_hw, 32)
            nc.scalar.activation(hw[:, 3:4], hw[:, 1:2], ACT.Exp)
            act.wait_ge(negw_ready, 1)
            act.wait_ge(dist_ready, 1)
            nc.scalar.activation(dist, dist, ACT.Exp, bias=hw[:, 1:2], scale=hw[:, 2:3]
                                 ).then_inc(e_ready, 1)

            def high(i):
                act.wait_ge(qk_psum, i + 1)
                nc.scalar.copy(parts[:, i // 2, i % 2, 0, :], bank[:, front_bank(("q", "k")[i % 2], i // 2), :]
                               ).then_inc(qk_hi, 1)

            def mid(i):
                act.wait_ge(qk_res, i + 1)
                nc.scalar.copy(parts[:, i // 2, i % 2, 1, :], residue[:, i % 2, :]).then_inc(qk_mid, 1)

            def front(name, b):
                if name == "turn":
                    act.wait_ge(xnT_psum, b + 1)
                    nc.scalar.copy(featA[:, b, :], bank[:, front_bank("turn", b), :]).then_inc(xnT_ready, 1)
                elif name == "q":
                    high(2 * b)
                elif name == "k":
                    high(2 * b + 1)
                    mid(2 * b)
                elif name == ("v" if b else "parts"):
                    mid(2 * b + 1)
                elif name in SIDE[:5]:
                    n = SIDE.index(name)
                    dst, cols = ((vecT[:, :], VEC_ROWS), (wT[:, 0:4, :].rearrange("p a d -> p (a d)"), 4 * D),
                                 (wT[:, 4:6, :].rearrange("p a d -> p (a d)"), 2 * D),
                                 (ctxT[:, :, :].rearrange("p b s -> p (b s)"), B * CL),
                                 (kpT[:, :, :].rearrange("p b s -> p (b s)"), B * CL))[n]
                    act.wait_ge(side_psum, n + 1)
                    nc.scalar.copy(dst, bank[:, SPARE, 0:cols]).then_inc(side_ready, 1)

            def stage(name, b):
                low, high = stage_banks(b)
                if name in ("context_turn", "xnorm_turn", "xcontext"):
                    act.wait_ge(d_psum[name], b + 1)
                    nc.scalar.copy(featA[:, b, :], low).then_inc(d_out[name], 1)
                elif name == "xquery":
                    act.wait_ge(d_psum[name], b + 1)
                    nc.scalar.activation(featB[:, b, :], high, ACT.Identity,
                                         bias=vecT[:, ROW_XBQ:ROW_XBQ + 1]).then_inc(d_out[name], 1)
                elif name == "xscore":
                    act.wait_ge(xmax_ready, b + 1)
                    for q in range(QT):
                        t = b * QT + q
                        last = nc.scalar.activation(xprob[:, b, q * P:q * P + CL], low[:, q * P:q * P + CL],
                                                    ACT.Exp, bias=xmax[:, t:t + 1], scale=X_SCALE,
                                                    accum_out=xsum[:, t:t + 1])
                    last.then_inc(d_out[name], 1)
                elif name == "fnorm_turn":
                    act.wait_ge(d_psum[name], b + 1)
                    nc.scalar.activation(featB[:, b, :], low, ACT.Identity,
                                         bias=vecT[:, ROW_LN_BIAS:ROW_LN_BIAS + 1],
                                         scale=vecT[:, ROW_LN_SCALE:ROW_LN_SCALE + 1]).then_inc(d_out[name], 1)
                elif name == "xattn":
                    act.wait_ge(d_psum[name], b + 1)
                    nc.scalar.activation(xat[:, b, :], high, ACT.Identity,
                                         bias=vecT[:, ROW_ATTN_B:ROW_ATTN_B + 1]).then_inc(d_out[name], 1)

            for name, slot in BEFORE:
                front(name, slot)

            def rectify(b, s):
                n = (s // HG % QT + 1) * P
                act.wait_ge(score_ready, b * STEPS + s + 1)
                nc.scalar.activation(bank[:, s % 4, 0:n], bank[:, s % 4, 0:n], ACT.Relu).then_inc(rectified, 1)

            def batch(b, last_batch):
                for s, u, g, qt, h in steps():
                    n = (qt + 1) * P
                    if s % 2 == 0:
                        if s + RECTIFY_AHEAD < STEPS:
                            rectify(b, s + RECTIFY_AHEAD)
                        elif not last_batch:
                            rectify(b + 1, s + RECTIFY_AHEAD - STEPS)
                    act.wait_ge(turned, b * STEPS + s + 1)
                    if s % HG == 0:
                        wait_batch(act, pv_done, b, UNITS, u - 1)
                    nc.scalar.activation(probT[:, (u % 2) * HG + s % HG, 0:n], bank[:, 4 + s % 2, 0:n],
                                         ACT.Exp, scale=-1.0 if s % 2 else 1.0).then_inc(exped, 1)
                    if s % HG == 3:
                        o_copy(b, u - 1)
                    if s % HG == 0:
                        ctx_save(b, u - 2)
                    for name, slot in beside(b, s, ACT_DELAY):
                        (front if b == 0 else stage)(name, slot)

            for s in range(1, RECTIFY_AHEAD, 2):
                rectify(0, s)
            batch(0, False)
            with act.Fori(1, B - 1) as b:
                batch(b, False)
            batch(B - 1, True)
            ctx_save(B, -2)
            o_copy(B, -1)
            ctx_save(B, -1)

            def tick(i):
                if i < E:
                    if i >= 2:
                        act.wait_ge(down_psum, i - 1)
                    for c in range(FC):
                        act.wait_ge(up_psum, i * FC + c // 2 * 2 + 2)
                        nc.scalar.activation(hid[:, (i % 2) * FC + c, :],
                                             bank[:, 4 + c // 2, (c % 2) * MB * P:(c % 2 + 1) * MB * P], ACT.Gelu,
                                             bias=vecT[:, ROW_B1 + i * FC + c:ROW_B1 + i * FC + c + 1]
                                             ).then_inc(hid_ready, 1)
                if 2 <= i < E + 2:
                    act.wait_ge(pre_ready, i - 1)
                    if i >= 4:
                        act.wait_ge(y_ready, i - 3)
                    nc.scalar.activation(act_out[:, i % 2, :], pre[:, i % 2, :], ACT.Gelu).then_inc(act_ready, 1)

            for what, which in after_attention():
                if what == "stage":
                    for b in range(HOSTED, B):
                        stage(which, b)
                else:
                    tick(which)

        @block.vector
        def _(dve):
            chain = [0]

            def link(ins):
                chain[0] += 1
                ins.then_inc(dve_step, 1)
                dve.wait_ge(dve_step, chain[0])

            def layer_norm_stats(k, b):
                for q in range(QT):
                    last = dve.bn_stats(stats[:, q, :], res[:, b * QT + q, :])
                link(last)
                for q in range(QT):
                    last = dve.bn_aggr(mv[:, b * QT + q, :], stats[:, q, :])
                last.then_inc(ln_stats[k], 1)
                dve.wait_ge(ln_stats[k], b + 1)

            def layer_norm_apply(k, b):
                dst = flat if k == 2 else norm
                dve.wait_ge(ln_rstd[k], b + 1)
                for q in range(QT):
                    t = b * QT + q
                    dve.tensor_scalar(dst[:, t, :], res[:, t, :], mv[:, t, 0:1], rstd[:, t:t + 1],
                                      ALU.subtract, ALU.mult).then_inc(ln_done[k], 1)

            dve.memset(strip[:, 0:P - 1], 0.0)
            dve.memset(strip[:, STRIP - 1:STRIP], 0.0)
            dve.memset(v_all[:, :, :, :, HD:VW].rearrange("p b k h w -> p (b k h w)"), 1.0)
            dve.memset(bank[:, 6, 0:P], 0.0).then_inc(o_zero, 1)
            dve.wait_ge(ld_hw, 32)
            dve.tensor_scalar(hw[:, 2:3], hw[:, 0:1], -1.0, None, ALU.mult).then_inc(negw_ready, 1)
            dve.wait_ge(ld_x[0], 16)
            layer_norm_stats(0, 0)
            dve.wait_ge(e_ready, 1)
            dve.tensor_scalar(hw[:, 4:5], hw[:, 3:4], 1.0, SCORE_SCALE, ALU.add, ALU.mult)
            link(dve.tensor_scalar(dist, dist, 1.0, None, ALU.add))
            dve.reciprocal(dist[:, 0:N // 2], dist[:, 0:N // 2])
            layer_norm_apply(0, 0)
            link(dve.reciprocal(dist[:, N // 2:N], dist[:, N // 2:N]))
            dve.tensor_scalar(strip[:, P - 1:P - 1 + N], dist, hw[:, 4:5], None, ALU.mult).then_inc(strip_ready, 1)

            def low_part(i):
                dve.wait_ge(qk_mid, i + 1)
                dve.tensor_tensor(parts[:, 0, i, 2, :], residue[:, i, :], parts[:, 0, i, 1, :],
                                  ALU.subtract).then_inc(qk_lo, 1)

            def front(name, b):
                if name == "stats":
                    dve.wait_ge(ld_x[b], 16)
                    layer_norm_stats(0, b)
                elif name == "norm":
                    layer_norm_apply(0, b)
                elif name in ("q", "k"):
                    i = 2 * b + (name == "k")
                    dve.wait_ge(qk_hi, i + 1)
                    if i >= 2:
                        dve.wait_ge(qk_lo, i - 1)
                    dve.tensor_tensor(residue[:, i % 2, :], bank[:, front_bank(name, b), :],
                                      parts[:, b, i % 2, 0, :], ALU.subtract).then_inc(qk_res, 1)
                    if b == 0 and name == "k":
                        low_part(0)
                elif name == "parts" and b == 0:
                    low_part(1)
                elif name == "v":
                    dve.wait_ge(v_psum, b + 1)
                    dve.tensor_copy(v_all[:, b, :, :, 0:HD].rearrange("p k h w -> p (k h) w"),
                                    bank[:, front_bank(name, b), :].rearrange("p (k h w) -> p (k h) w", h=H, w=HD)
                                    ).then_inc(v_ready, 1)
                elif name == "xvalues":
                    dve.wait_ge(side_psum, 6)
                    dve.wait_ge(ld_bc, 64)
                    dve.tensor_tensor(vp[:, :, :], bank[0:CL, SPARE, :].rearrange("p (b d) -> p b d", d=D),
                                      bv_b[0:CL, :].rearrange("p (o d) -> p o d", o=1).to_broadcast([CL, B, D]),
                                      ALU.add).then_inc(side_ready, 1)

            def stage(name, b):
                ts = slice(b * QT, (b + 1) * QT)
                low, high = stage_banks(b)
                if name == "context":
                    dve.wait_ge(ctx_saved, (b + 1) * UNITS)
                    link(dve.reciprocal(ctx_rec[:, ts, :], ctx_sum[:, ts, :, HD]))
                    dve.tensor_tensor(norm[:, ts, :].rearrange("p t (h w) -> p (t h) w", w=HD),
                                      ctx_sum[:, ts, :, 0:HD].rearrange("p t h w -> p (t h) w"),
                                      ctx_rec[:, ts, :].rearrange("p t (h o) -> p (t h) o", o=1
                                                                  ).to_broadcast([P, QT * H, HD]),
                                      ALU.mult).then_inc(d_out[name], 1)
                elif name == "attn_out":
                    dve.wait_ge(d_psum[name], b + 1)
                    dve.wait_ge(biased, (b + 1) * QT)
                    link(dve.tensor_tensor(res[:, ts, :], high.rearrange("p (t d) -> p t d", d=D),
                                           res[:, ts, :], ALU.add))
                    layer_norm_stats(1, b)
                elif name == "xnorm":
                    layer_norm_apply(1, b)
                elif name == "xscore":
                    dve.wait_ge(d_psum[name], b + 1)
                    link(dve.tensor_reduce(xmax[:, ts], low.rearrange("p (t k) -> p t k", k=P)[:, :, 0:CL],
                                           AX.X, ALU.max))
                    dve.tensor_scalar(xmax[:, ts], xmax[:, ts], -X_SCALE, None, ALU.mult
                                      ).then_inc(xmax_ready, 1)
                elif name == "xprob_turn":
                    dve.wait_ge(d_psum[name], b + 1)
                    dve.tensor_copy(xprobT[:, b, :], high[0:CL, :]).then_inc(d_out[name], 1)
                elif name == "xout":
                    dve.wait_ge(d_out["xscore"], b + 1)
                    link(dve.reciprocal(xrec[:, ts], xsum[:, ts]))
                    dve.wait_ge(xbiased[b], QT)
                    dve.wait_ge(d_psum[name], b + 1)
                    for q in range(QT):
                        t = b * QT + q
                        last = dve.scalar_tensor_tensor(out=res[:, t, :], in0=high[:, q * P:(q + 1) * P],
                                                        scalar=xrec[:, t:t + 1], in1=res[:, t, :],
                                                        op0=ALU.mult, op1=ALU.add)
                    link(last)
                    layer_norm_stats(2, b)
                elif name == "flat":
                    layer_norm_apply(2, b)
                elif name == "fnorm":
                    dve.wait_ge(ln_rstd[3], b + 1)
                    for t in range(b * QT, (b + 1) * QT):
                        dve.wait_ge(ln_done[2], t + 1)
                        dve.tensor_scalar(norm[:, t, :], flat[:, t, :], rstd2[:, t:t + 1], None, ALU.mult
                                          ).then_inc(ln_done[3], 1)

            for name, slot in BEFORE[2:]:
                front(name, slot)

            def shift(b, s):
                n = (s // HG % QT + 1) * P
                wait_batch(dve, gated, b, STEPS, s + 1)
                dve.tensor_scalar(zbuf[:, s % ZS, 0:n], zbuf[:, s % ZS, 0:n], 0.0, rowmax[:, s % ZS:s % ZS + 1],
                                  ALU.max, ALU.subtract).then_inc(shifted_even, 1)

            def batch(b):
                for s, u, g, qt, h in steps():
                    n = (qt + 1) * P
                    if isinstance(b, int) and b == 0 and s % (QT * HG) == 0:
                        dve.wait_ge(gate_loaded[g], 16)
                    wait_batch(dve, turned, b, STEPS, s - ZS + 1)
                    if s % 2 == 1:
                        dve.wait_ge(rectified, b * (STEPS // 2) + s // 2 + 1)
                    else:
                        dve.wait_ge(score_ready, b * STEPS + s + 1)
                    hold(dve, dve_passed)
                    dve.tensor_tensor_reduce(zbuf[:, s % ZS, 0:n], bank[:, s % 4, 0:n],
                                             gate[:, h, 0:n][:, ::-1], 1.0, 0.0, ALU.mult, ALU.max,
                                             rowmax[:, s % ZS:s % ZS + 1]).then_inc(gated, 1)
                    if s % 2 == 1:
                        shift(b, s - 1)
                    for name, slot in beside(b, s, DVE_DELAY):
                        (front if b == 0 else stage)(name, slot)

            batch(0)
            with dve.Fori(1, B - 1) as b:
                batch(b)
            batch(B - 1)

            def tick(i):
                if 2 <= i < E + 2:
                    f = i - 2
                    dve.wait_ge(next_psum, f + 1)
                    if f >= 2:
                        dve.wait_ge(act_ready, f - 1)
                    dve.tensor_tensor(pre[:, f % 2, :].rearrange("p (m d) -> p m d", d=D),
                                      bank[:, 7, 0:MB * D].rearrange("p (m d) -> p m d", d=D),
                                      nb_b[:, :].rearrange("p (o d) -> p o d", o=1).to_broadcast([P, MB, D]),
                                      ALU.add).then_inc(pre_ready, 1)
                if i >= 3:
                    f = i - 3
                    dve.wait_ge(act_ready, f + 1)
                    if f >= 2:
                        dve.wait_ge(y_stored[f % 2], 16 * (f // 2))
                    dve.tensor_tensor(y_out[:, f % 2, :].rearrange("p (m d) -> p m d", d=D),
                                      act_out[:, f % 2, :].rearrange("p (m d) -> p m d", d=D),
                                      res_v[:, f // QT * MB:(f // QT + 1) * MB, f % QT, :], ALU.add
                                      ).then_inc(y_ready, 1)
                if 1 <= i < E + 1:
                    f = i - 1
                    dve.wait_ge(down_psum, f + 1)
                    if f >= 2:
                        dve.wait_ge(next_psum, f - 1)
                    dve.tensor_scalar(eo[:, f % 2, :], bank[:, 6, 0:MB * P],
                                      vecT[:, ROW_B2 + f:ROW_B2 + f + 1], None, ALU.add).then_inc(eo_ready, 1)

            for what, which in after_attention():
                if what == "stage":
                    for b in range(HOSTED, B):
                        stage(which, b)
                else:
                    tick(which)

        @block.tensor
        def _(pe):
            mm, turn = nc.tensor.matmul, nc.tensor.transpose
            pe.wait_ge(ident_ready, 1)
            for _ in range(WARM_UP):
                mm(bank[:, 3, 0:P], ident[:, :], ident[:, :], start=True, stop=True)
            pe.wait_ge(ld_proj, 48)

            def front(name, b):
                if name == "turn":
                    if b >= 2:
                        pe.wait_ge(v_ready, b)
                    for q in range(QT):
                        pe.wait_ge(ln_done[0], b * QT + q + 1)
                        last = turn(bank[:, front_bank(name, b), q * P:(q + 1) * P], norm[:, b * QT + q, :],
                                    ident[:, :])
                    last.then_inc(xnT_psum, 1)
                elif name in ("q", "k"):
                    pe.wait_ge(xnT_ready, b + 1)
                    if b >= 2 and name == "k":
                        pe.wait_ge(qk_res, 2 * b + 1)
                    mm(bank[:, front_bank(name, b), :], (wq if name == "q" else wk)[:, :], featA[:, b, :],
                       start=True, stop=True).then_inc(qk_psum, 1)
                elif name == "v":
                    if b >= 2:
                        pe.wait_ge(qk_res, 2 * b + 2)
                    elif b:
                        pe.wait_ge(v_ready, b)
                    for q in range(QT):
                        last = mm(bank[:, front_bank(name, b), q * P:(q + 1) * P],
                                  featA[:, b, q * P:(q + 1) * P], wv[:, :], start=True, stop=True)
                    last.then_inc(v_psum, 1)
                elif name in SIDE:
                    n = SIDE.index(name)
                    if n:
                        pe.wait_ge(side_ready, n)
                    if name == "vectors":
                        pe.wait_ge(v_ready, B)
                        pe.wait_ge(ld_vec, 96)
                        last = turn(bank[:, SPARE, 0:VEC_ROWS], vecs[:, :], ident[0:VEC_ROWS, 0:VEC_ROWS])
                    elif name == "weights":
                        pe.wait_ge(ld_raw, 96)
                        for i in range(4):
                            last = turn(bank[:, SPARE, i * P:(i + 1) * P], raw_w[:, i, :], ident[:, :])
                    elif name == "weights2":
                        for i in range(2):
                            last = turn(bank[:, SPARE, i * P:(i + 1) * P], raw_w[:, 4 + i, :], ident[:, :])
                    elif name == "context":
                        pe.wait_ge(ld_ctx, 16 * B)
                        for i in range(B):
                            last = turn(bank[:, SPARE, i * CL:(i + 1) * CL], ctx_in[:, i, :], ident[0:CL, 0:CL])
                    elif name == "xkeys":
                        last = mm(bank[:, SPARE, 0:B * CL], wT[:, XWK, :],
                                  ctxT[:, :, :].rearrange("p b s -> p (b s)"), start=True, stop=True)
                    elif name == "xvalues":
                        for i in range(B):
                            last = mm(bank[0:CL, SPARE, i * P:(i + 1) * P], ctxT[:, i, :], wT[:, XWV, :],
                                      start=True, stop=True)
                    last.then_inc(side_psum, 1)

            read_out = dict(d_out, attn_out=ln_stats[1], xout=ln_stats[2])
            bank_user = [None]

            def stage(name, b):
                if name in ("context", "xnorm", "flat", "fnorm"):
                    return
                low, high = stage_banks(b)
                tiles = [(slice(q * P, (q + 1) * P), b * QT + q) for q in range(QT)]
                if b < HOSTED:
                    if bank_user[0]:
                        pe.wait_ge(read_out[bank_user[0][0]], bank_user[0][1] + 1)
                    bank_user[0] = (name, b)
                if name in ("context_turn", "xnorm_turn", "fnorm_turn"):
                    if name == "context_turn":
                        pe.wait_ge(d_out["context"], b + 1)
                    for cols, t in tiles:
                        if name != "context_turn":
                            pe.wait_ge(ln_done[1 if name == "xnorm_turn" else 3], t + 1)
                        last = turn(low[:, cols], norm[:, t, :], ident[:, :])
                elif name == "attn_out":
                    if b == 0:
                        pe.wait_ge(ld_wo, 16)
                    pe.wait_ge(d_out["context_turn"], b + 1)
                    for cols, t in tiles:
                        last = mm(high[:, cols], featA[:, b, cols], wo[:, :], start=True, stop=True)
                elif name == "xquery":
                    pe.wait_ge(d_out["xnorm_turn"], b + 1)
                    last = mm(high, wT[:, XWQ, :], featA[:, b, :], start=True, stop=True)
                elif name == "xscore":
                    pe.wait_ge(d_out["xquery"], b + 1)
                    for cols, t in tiles:
                        last = mm(low[:, cols.start:cols.start + CL], featB[:, b, cols], kpT[:, b, :],
                                  start=True, stop=True)
                elif name == "xprob_turn":
                    pe.wait_ge(d_out["xscore"], b + 1)
                    for cols, t in tiles:
                        last = turn(high[0:CL, cols], xprob[:, b, cols.start:cols.start + CL], ident[:, :])
                elif name == "xcontext":
                    pe.wait_ge(d_out["xprob_turn"], b + 1)
                    last = mm(low, vp[:, b, :], xprobT[:, b, :], start=True, stop=True)
                elif name == "xout":
                    pe.wait_ge(d_out["xcontext"], b + 1)
                    for cols, t in tiles:
                        last = mm(high[:, cols], featA[:, b, cols], wT[:, XWO, :], start=True, stop=True)
                elif name == "xattn":
                    pe.wait_ge(d_out["fnorm_turn"], b + 1)
                    mm(high, wT[:, FAW, :], featB[:, b, :], start=True, stop=False, skip_group_check=True)
                    for cols, t in tiles:
                        last = mm(high[:, cols], flat[:, t, :], ident[:, :], start=False,
                                  stop=(t % QT == QT - 1), skip_group_check=True)
                last.then_inc(d_psum[name], 1)

            for name, slot in BEFORE:
                front(name, slot)
            pe.wait_ge(o_zero, 1)

            plan = list(steps())

            def scores(b, s):
                _, u, g, qt, h = plan[s]
                n, i, j = (qt + 1) * P, h % 2, h // 2
                if s % (QT * HG) == 0:
                    pe.wait_ge(stack_loaded[g], b * 64 + 64)
                wait_batch(pe, gated, b, STEPS, s - 3)
                r = slice(64 * i, 64 * i + SLOTS * HD)
                mm(bank[:, s % 4, 0:n], qk_stack[r, 0, j, qt * P:(qt + 1) * P], qk_stack[r, 1, j, 0:n],
                   start=True, stop=True).then_inc(score_ready, 1)

            def turn_step(b, s):
                if isinstance(b, int) and b * STEPS + s < 0:
                    return
                qt = s // HG % QT
                wait_batch(pe, shifted_odd if s % 2 else shifted_even, b, STEPS // 2, s // 2 + 1)
                wait_batch(pe, exped, b, STEPS, s - 1)
                for k in range(qt + 1):
                    last = turn(bank[:, 4 + s % 2, k * P:(k + 1) * P], zbuf[:, s % ZS, k * P:(k + 1) * P],
                                ident[:, :])
                last.then_inc(turned, 1)

            def values(b, u, part):
                if isinstance(b, int) and b * UNITS + u < 0:
                    return
                g, qt = u % UNITS // QT, u % QT
                blocks = VALUE_BLOCKS[qt][part]
                if not blocks:
                    return
                if blocks[0] == 0:
                    wait_batch(pe, exped, b, STEPS, HG * (u + 1))
                    wait_batch(pe, ctx_saved, b, UNITS, u)
                    if qt == 0:
                        wait_batch(pe, v_copied, b, G, g + 1)
                if blocks[-1] == qt:
                    wait_batch(pe, masked, b, UNITS, u + 1)
                for k in blocks:
                    for i in range(HG):
                        last = mm(bank[32 * i:32 * i + VW, 6, 0:P], v_cur[:, k, g * HG + i, :],
                                  probT[:, (u % 2) * HG + i, k * P:(k + 1) * P],
                                  start=(k == 0), stop=(k == qt))
                if blocks[-1] == qt:
                    last.then_inc(pv_done, 1)

            def turn_context(b, u):
                if isinstance(b, int) and b * UNITS + u < 0:
                    return
                wait_batch(pe, o_copied, b, UNITS, u + 1)
                turn(bank[:, 6, P:2 * P], o_sb[:, u % 2, :], ident[:, :]).then_inc(o_turned, 1)

            def batch(b, last_batch):
                for s in range(STEPS):
                    if s + SCORES_AHEAD < STEPS:
                        scores(b, s + SCORES_AHEAD)
                    elif not last_batch:
                        scores(b + 1, s + SCORES_AHEAD - STEPS)
                    turn_step(b, s - TURN_LAG)
                    if s % HG < 2:
                        values(b, s // HG - 2, s % HG)
                    if s % HG == 2:
                        turn_context(b, s // HG - 2)
                    for name, slot in beside(b, s, PE_DELAY):
                        (front if b == 0 else stage)(name, slot)

            pe.wait_ge(qk_res, 4)
            for s in range(SCORES_AHEAD):
                scores(0, s)
            batch(0, False)
            with pe.Fori(1, B - 1) as b:
                batch(b, False)
            batch(B - 1, True)
            for s in range(-TURN_LAG, 0):
                turn_step(B, s)
            for u in (-2, -1):
                for part in range(2):
                    values(B, u, part)
                turn_context(B, u)

            def tick(i):
                if i < E:
                    p, q = i // QT, i % QT
                    if i == 0:
                        pe.wait_ge(ld_ffn, 32)
                    pe.wait_ge(d_out["xattn"], (p + 1) * MB)
                    for c in range(FC):
                        if i >= 1 and c % 2 == 0:
                            pe.wait_ge(hid_ready, (i - 1) * FC + c + 2)
                        mm(bank[:, 4 + c // 2, (c % 2) * MB * P:(c % 2 + 1) * MB * P], w1[:, i, c * P:(c + 1) * P],
                           xat[:, p * MB:(p + 1) * MB, q * P:(q + 1) * P], start=True, stop=True
                           ).then_inc(up_psum, 1)
                if 2 <= i < E + 2:
                    f = i - 2
                    pe.wait_ge(eo_ready, f + 1)
                    if f >= 1:
                        pe.wait_ge(pre_ready, f)
                    for m in range(MB):
                        last = mm(bank[:, 7, m * P:(m + 1) * P], eo[:, f % 2, m * P:(m + 1) * P],
                                  wT[:, FNW, :], start=True, stop=True)
                    last.then_inc(next_psum, 1)
                if 1 <= i < E + 1:
                    f = i - 1
                    if f >= 1:
                        pe.wait_ge(eo_ready, f)
                    for c in range(FC):
                        pe.wait_ge(hid_ready, f * FC + c + 1)
                        last = mm(bank[:, 6, 0:MB * P], w2[:, f, c, :], hid[:, (f % 2) * FC + c, :],
                                  start=(c == 0), stop=(c == FC - 1))
                    last.then_inc(down_psum, 1)

            for what, which in after_attention():
                if what == "stage":
                    for b in range(HOSTED, B):
                        stage(which, b)
                else:
                    tick(which)


_INS = ['x', 'ctx_1024', 'L0_attn_Wq', 'L0_attn_Wk', 'L0_attn_Wv', 'L0_attn_Wo', 'L0_attn_bo', 'L0_attn_w',
        'L0_attn_v', 'L0_xattn_Wk', 'L0_xattn_Wv', 'L0_xattn_bv', 'L0_xattn_Wq', 'L0_xattn_bq', 'L0_xattn_Wo',
        'L0_xattn_bo', 'L0_ffn_ln_scale', 'L0_ffn_ln_bias', 'L0_ffn_attn_w', 'L0_ffn_attn_b', 'L0_ffn_w1',
        'L0_ffn_b1', 'L0_ffn_w2', 'L0_ffn_b2', 'L0_ffn_next_w', 'L0_ffn_next_b']


def kernel(**inputs):
    import numpy as _np
    import concourse.bacc as _bacc
    from concourse import mybir as _mybir
    from concourse.bass_utils import run_bass_kernel_spmd as _run

    nc = _bacc.Bacc("TRN2", target_bir_lowering=False, num_devices=1)
    arrays, args = {}, []
    for name in _INS:
        a = _np.ascontiguousarray(inputs[name])
        arrays[f"in_{name}"] = a
        args.append(nc.dram_tensor(f"in_{name}", a.shape, _mybir.dt.from_np(a.dtype), kind="ExternalInput").ap())
    shape = tuple(inputs["x"].shape)
    args.append(nc.dram_tensor("out_x", shape, _mybir.dt.float32, kind="ExternalOutput").ap())
    decoder_kernel(nc, *args)
    r = _run(nc, [arrays], core_ids=[0])
    return r.results[0]["out_x"]
```
